# Optimizing a Trainium2 kernel written in Bass

```python
import numpy as np
import jax
import jax.numpy as jnp

def _softmax(x, axis=-1):
    return jax.nn.softmax(x, axis=axis)
def _gelu(x):
    return jax.nn.gelu(x, approximate=True)
def _silu(x):
    return jax.nn.silu(x)
def _sigmoid(x):
    return jax.nn.sigmoid(x)
def _layernorm(x, axis=-1, eps=1e-5):
    m = jnp.mean(x, axis=axis, keepdims=True)
    v = jnp.var(x, axis=axis, keepdims=True)
    return (x - m) / jnp.sqrt(v + eps)
def _scatter_add(tgt, idx, src, axis=0):
    return tgt.at[idx].add(src)
def _segment_sum(src, seg, n):
    return jax.ops.segment_sum(src, seg, n)

kernel_name = 'mk_conv_preact_d2_conv_nchw8_6ba772'

def setup_inputs(seed: int = 0):
    np.random.seed(seed)
    _w = jnp.asarray
    def _rec_inputs():
        import jax
        import jax.numpy as jnp
        _gk = jax.random.key(seed)
        x = -0.0002928 + 1 * jax.random.normal(jax.random.fold_in(_gk, 1), (8, 8, 256, 256), jnp.float32)
        return x
    x = _rec_inputs()
    def _L0_conv_setup():
        import jax, jax.numpy as jnp
        import numpy as np
        G = 4
        SC = 2
        WID = 10
        M1 = 12
        M2 = 12
        B = 8
        H = 256
        W = 256

        def _gconv1x1(x, w, b):
            Bb, _, Hh, Ww = x.shape
            xg = x.reshape(Bb, G, -1, Hh, Ww)
            y = jnp.einsum('bgihw,goi->bgohw', xg, w).reshape(Bb, -1, Hh, Ww)
            return y + b[None, :, None, None]

        def _gswish(x, beta):
            Bb, C, Hh, Ww = x.shape
            xg = x.reshape(Bb, G, -1, Hh, Ww)
            sp = jax.nn.softplus(beta)[None, :, None, None, None]
            return (xg * jax.nn.sigmoid(xg * sp) / 1.1).reshape(Bb, C, Hh, Ww)

        def _spectral_conv(x, w1, w2):
            Bb, _, Hh, Ww = x.shape
            Wf = Ww // 2 + 1
            xf = jnp.fft.rfft2(x).reshape(Bb, G, WID, Hh, Wf)
            w1c = w1[..., 0] + 1j * w1[..., 1]
            w2c = w2[..., 0] + 1j * w2[..., 1]
            lo = jnp.einsum('bgixy,gioxy->bgoxy', xf[:, :, :, :M1, :M2], w1c)
            hi = jnp.einsum('bgixy,gioxy->bgoxy', xf[:, :, :, Hh - M1:, :M2], w2c)
            out_ft = jnp.zeros((Bb, G, WID, Hh, Wf), jnp.complex64)
            out_ft = out_ft.at[:, :, :, :M1, :M2].set(lo)
            out_ft = out_ft.at[:, :, :, Hh - M1:, :M2].set(hi)
            return jnp.fft.irfft2(out_ft.reshape(Bb, G * WID, Hh, Wf), s=(Hh, Ww))
        key = jax.random.key(seed)
        ks = jax.random.split(key, 12)
        scale = 1.0 / (WID * WID)
        x = jax.random.normal(ks[0], (B, G * SC, H, W), jnp.float32)
        fc0_w = jax.random.normal(ks[1], (G, WID, SC + 2), jnp.float32) * 0.1
        fc0_b = jax.random.normal(ks[2], (G * WID,), jnp.float32) * 0.01
        w_w = jax.random.normal(ks[3], (4, G, WID, WID), jnp.float32) * 0.1
        w_b = jax.random.normal(ks[4], (4, G * WID), jnp.float32) * 0.01
        sp_w1 = scale * jax.random.uniform(ks[5], (4, G, WID, WID, M1, M2, 2), jnp.float32)
        sp_w2 = scale * jax.random.uniform(ks[6], (4, G, WID, WID, M1, M2, 2), jnp.float32)
        betas = jnp.full((4, G), 0.5, jnp.float32)
        fc1_w = jax.random.normal(ks[7], (G, 128, WID), jnp.float32) * 0.05
        fc1_b = jax.random.normal(ks[8], (G * 128,), jnp.float32) * 0.01
        fc2_w = jax.random.normal(ks[9], (G, SC, 128), jnp.float32) * 0.05
        fc2_b = jax.random.normal(ks[10], (G * SC,), jnp.float32) * 0.01
        return {'x': x, 'fc0_w': fc0_w, 'fc0_b': fc0_b, 'w_w': w_w, 'w_b': w_b, 'sp_w1': sp_w1, 'sp_w2': sp_w2, 'betas': betas, 'fc1_w': fc1_w, 'fc1_b': fc1_b, 'fc2_w': fc2_w, 'fc2_b': fc2_b}
    _L0_conv_all = _L0_conv_setup()
    _L0_conv_in = {k: v for k, v in _L0_conv_all.items() if k in ('fc0_w', 'fc0_b', 'w_w', 'w_b', 'sp_w1', 'sp_w2', 'betas', 'fc1_w', 'fc1_b', 'fc2_w', 'fc2_b', )}
    del _L0_conv_all

    def _L1_conv_setup():
        import jax, jax.numpy as jnp
        import numpy as np
        from jax import lax
        R = 4
        C_IN = 8
        D_MODEL = C_IN * R * R
        D_STATE = 64
        D_INNER = 2 * D_MODEL
        D_CONV = 4
        DT_RANK = (D_MODEL + 15) // 16
        B, H, W = (16, 256, 256)

        def _pixel_unshuffle(x, r):
            b, c, h, w = x.shape
            x = x.reshape(b, c, h // r, r, w // r, r)
            x = x.transpose(0, 1, 3, 5, 2, 4)
            return x.reshape(b, c * r * r, h // r, w // r)

        def _pixel_shuffle(x, r):
            b, cr, h, w = x.shape
            c = cr // (r * r)
            x = x.reshape(b, c, r, r, h, w)
            x = x.transpose(0, 1, 4, 2, 5, 3)
            return x.reshape(b, c, h * r, w * r)

        def _layernorm(x, gamma, beta, eps=1e-05):
            mu = jnp.mean(x, axis=-1, keepdims=True)
            var = jnp.mean(jnp.square(x - mu), axis=-1, keepdims=True)
            return (x - mu) * lax.rsqrt(var + eps) * gamma + beta

        def _mamba(u, in_proj_w, conv_w, conv_b, x_proj_w, dt_proj_w, dt_proj_b, A_log, D, out_proj_w):
            xz = jnp.einsum('bld,ed->ble', u, in_proj_w)
            x_in, z = jnp.split(xz, 2, axis=-1)
            xc = x_in.transpose(0, 2, 1)
            xc = jnp.pad(xc, ((0, 0), (0, 0), (D_CONV - 1, 0)))
            xc = lax.conv_general_dilated(xc, conv_w, (1,), 'VALID', dimension_numbers=('NCH', 'OIH', 'NCH'), feature_group_count=D_INNER)
            xc = jax.nn.silu(xc.transpose(0, 2, 1) + conv_b)
            x_dbl = jnp.einsum('bld,ed->ble', xc, x_proj_w)
            dt, Bc, Cc = jnp.split(x_dbl, [DT_RANK, DT_RANK + D_STATE], axis=-1)
            dt = jax.nn.softplus(jnp.einsum('blr,dr->bld', dt, dt_proj_w) + dt_proj_b)
            A = -jnp.exp(A_log)

            def step(h, inputs):
                dt_t, x_t, B_t, C_t = inputs
                h = h * jnp.exp(dt_t[..., None] * A) + (dt_t * x_t)[..., None] * B_t[:, None, :]
                y = jnp.einsum('bds,bs->bd', h, C_t)
                return (h, y)
            h0 = jnp.zeros((u.shape[0], D_INNER, D_STATE), u.dtype)
            _, ys = lax.scan(step, h0, (dt.transpose(1, 0, 2), xc.transpose(1, 0, 2), Bc.transpose(1, 0, 2), Cc.transpose(1, 0, 2)))
            y = ys.transpose(1, 0, 2) + xc * D
            y = y * jax.nn.silu(z)
            return jnp.einsum('bld,ed->ble', y, out_proj_w)
        key = jax.random.key(seed)
        ks = jax.random.split(key, 12)

        def rn(k, shape, scale):
            return jax.random.normal(k, shape, dtype=jnp.float32) * scale
        inp = {'x': rn(ks[0], (B, C_IN, H, W), 1.0), 'ln_gamma': jnp.ones((D_MODEL,), jnp.float32), 'ln_beta': jnp.zeros((D_MODEL,), jnp.float32), 'in_proj_w': rn(ks[1], (2 * D_INNER, D_MODEL), D_MODEL ** (-0.5)), 'conv_w': rn(ks[2], (D_INNER, 1, D_CONV), D_CONV ** (-0.5)), 'conv_b': rn(ks[3], (D_INNER,), 0.02), 'x_proj_w': rn(ks[4], (DT_RANK + 2 * D_STATE, D_INNER), D_INNER ** (-0.5)), 'dt_proj_w': rn(ks[5], (D_INNER, DT_RANK), DT_RANK ** (-0.5)), 'dt_proj_b': rn(ks[6], (D_INNER,), 0.1), 'A_log': jnp.log(jnp.broadcast_to(jnp.arange(1, D_STATE + 1, dtype=jnp.float32), (D_INNER, D_STATE))), 'D': jnp.ones((D_INNER,), jnp.float32), 'out_proj_w': rn(ks[7], (D_MODEL, D_INNER), D_INNER ** (-0.5))}
        return inp
    _L1_conv_all = _L1_conv_setup()
    _L1_conv_in = {k: v for k, v in _L1_conv_all.items() if k in ('ln_gamma', 'ln_beta', 'in_proj_w', 'conv_w', 'conv_b', 'x_proj_w', 'dt_proj_w', 'dt_proj_b', 'A_log', 'D', 'out_proj_w', )}
    del _L1_conv_all

    return {
        "x": x,
        "L0_conv_fc0_w": _L0_conv_in["fc0_w"],
        "L0_conv_fc0_b": _L0_conv_in["fc0_b"],
        "L0_conv_w_w": _L0_conv_in["w_w"],
        "L0_conv_w_b": _L0_conv_in["w_b"],
        "L0_conv_sp_w1": _L0_conv_in["sp_w1"],
        "L0_conv_sp_w2": _L0_conv_in["sp_w2"],
        "L0_conv_betas": _L0_conv_in["betas"],
        "L0_conv_fc1_w": _L0_conv_in["fc1_w"],
        "L0_conv_fc1_b": _L0_conv_in["fc1_b"],
        "L0_conv_fc2_w": _L0_conv_in["fc2_w"],
        "L0_conv_fc2_b": _L0_conv_in["fc2_b"],
        "L1_conv_ln_gamma": _L1_conv_in["ln_gamma"],
        "L1_conv_ln_beta": _L1_conv_in["ln_beta"],
        "L1_conv_in_proj_w": _L1_conv_in["in_proj_w"],
        "L1_conv_conv_w": _L1_conv_in["conv_w"],
        "L1_conv_conv_b": _L1_conv_in["conv_b"],
        "L1_conv_x_proj_w": _L1_conv_in["x_proj_w"],
        "L1_conv_dt_proj_w": _L1_conv_in["dt_proj_w"],
        "L1_conv_dt_proj_b": _L1_conv_in["dt_proj_b"],
        "L1_conv_A_log": _L1_conv_in["A_log"],
        "L1_conv_D": _L1_conv_in["D"],
        "L1_conv_out_proj_w": _L1_conv_in["out_proj_w"],
    }

def reference(x, L0_conv_fc0_w, L0_conv_fc0_b, L0_conv_w_w, L0_conv_w_b, L0_conv_sp_w1, L0_conv_sp_w2, L0_conv_betas, L0_conv_fc1_w, L0_conv_fc1_b, L0_conv_fc2_w, L0_conv_fc2_b, L1_conv_ln_gamma, L1_conv_ln_beta, L1_conv_in_proj_w, L1_conv_conv_w, L1_conv_conv_b, L1_conv_x_proj_w, L1_conv_dt_proj_w, L1_conv_dt_proj_b, L1_conv_A_log, L1_conv_D, L1_conv_out_proj_w):
    import jax
    import jax.numpy as jnp
    def _L0_conv_ref(x, fc0_w, fc0_b, w_w, w_b, sp_w1, sp_w2, betas, fc1_w, fc1_b, fc2_w, fc2_b):
        import jax, jax.numpy as jnp
        import numpy as np
        G = 4
        SC = 2
        WID = 10
        M1 = 12
        M2 = 12
        B = 8
        H = 256
        W = 256

        def _gconv1x1(x, w, b):
            Bb, _, Hh, Ww = x.shape
            xg = x.reshape(Bb, G, -1, Hh, Ww)
            y = jnp.einsum('bgihw,goi->bgohw', xg, w).reshape(Bb, -1, Hh, Ww)
            return y + b[None, :, None, None]

        def _gswish(x, beta):
            Bb, C, Hh, Ww = x.shape
            xg = x.reshape(Bb, G, -1, Hh, Ww)
            sp = jax.nn.softplus(beta)[None, :, None, None, None]
            return (xg * jax.nn.sigmoid(xg * sp) / 1.1).reshape(Bb, C, Hh, Ww)

        def _spectral_conv(x, w1, w2):
            Bb, _, Hh, Ww = x.shape
            Wf = Ww // 2 + 1
            xf = jnp.fft.rfft2(x).reshape(Bb, G, WID, Hh, Wf)
            w1c = w1[..., 0] + 1j * w1[..., 1]
            w2c = w2[..., 0] + 1j * w2[..., 1]
            lo = jnp.einsum('bgixy,gioxy->bgoxy', xf[:, :, :, :M1, :M2], w1c)
            hi = jnp.einsum('bgixy,gioxy->bgoxy', xf[:, :, :, Hh - M1:, :M2], w2c)
            out_ft = jnp.zeros((Bb, G, WID, Hh, Wf), jnp.complex64)
            out_ft = out_ft.at[:, :, :, :M1, :M2].set(lo)
            out_ft = out_ft.at[:, :, :, Hh - M1:, :M2].set(hi)
            return jnp.fft.irfft2(out_ft.reshape(Bb, G * WID, Hh, Wf), s=(Hh, Ww))
        Bb, _, Hh, Ww = x.shape
        gridx = jnp.broadcast_to(jnp.linspace(0.0, 1.0, Hh)[:, None], (Hh, Ww))
        gridy = jnp.broadcast_to(jnp.linspace(0.0, 1.0, Ww)[None, :], (Hh, Ww))
        grid = jnp.stack([gridx, gridy], axis=0)
        xg = x.reshape(Bb, G, SC, Hh, Ww)
        gridb = jnp.broadcast_to(grid[None, None], (Bb, G, 2, Hh, Ww))
        h = jnp.concatenate([xg, gridb], axis=2).reshape(Bb, G * (SC + 2), Hh, Ww)
        h = _gconv1x1(h, fc0_w, fc0_b)
        for i in range(4):
            h1 = _spectral_conv(h, sp_w1[i], sp_w2[i])
            h2 = _gconv1x1(h, w_w[i], w_b[i])
            h = h1 + h2
            if i < 3:
                h = _gswish(h, betas[i])
        h = _gswish(_gconv1x1(h, fc1_w, fc1_b), betas[3])
        return _gconv1x1(h, fc2_w, fc2_b)

    def _L1_conv_ref(x, ln_gamma, ln_beta, in_proj_w, conv_w, conv_b, x_proj_w, dt_proj_w, dt_proj_b, A_log, D, out_proj_w):
        import jax, jax.numpy as jnp
        import numpy as np
        from jax import lax
        R = 4
        C_IN = 8
        D_MODEL = C_IN * R * R
        D_STATE = 64
        D_INNER = 2 * D_MODEL
        D_CONV = 4
        DT_RANK = (D_MODEL + 15) // 16
        B, H, W = (16, 256, 256)

        def _pixel_unshuffle(x, r):
            b, c, h, w = x.shape
            x = x.reshape(b, c, h // r, r, w // r, r)
            x = x.transpose(0, 1, 3, 5, 2, 4)
            return x.reshape(b, c * r * r, h // r, w // r)

        def _pixel_shuffle(x, r):
            b, cr, h, w = x.shape
            c = cr // (r * r)
            x = x.reshape(b, c, r, r, h, w)
            x = x.transpose(0, 1, 4, 2, 5, 3)
            return x.reshape(b, c, h * r, w * r)

        def _layernorm(x, gamma, beta, eps=1e-05):
            mu = jnp.mean(x, axis=-1, keepdims=True)
            var = jnp.mean(jnp.square(x - mu), axis=-1, keepdims=True)
            return (x - mu) * lax.rsqrt(var + eps) * gamma + beta

        def _mamba(u, in_proj_w, conv_w, conv_b, x_proj_w, dt_proj_w, dt_proj_b, A_log, D, out_proj_w):
            xz = jnp.einsum('bld,ed->ble', u, in_proj_w)
            x_in, z = jnp.split(xz, 2, axis=-1)
            xc = x_in.transpose(0, 2, 1)
            xc = jnp.pad(xc, ((0, 0), (0, 0), (D_CONV - 1, 0)))
            xc = lax.conv_general_dilated(xc, conv_w, (1,), 'VALID', dimension_numbers=('NCH', 'OIH', 'NCH'), feature_group_count=D_INNER)
            xc = jax.nn.silu(xc.transpose(0, 2, 1) + conv_b)
            x_dbl = jnp.einsum('bld,ed->ble', xc, x_proj_w)
            dt, Bc, Cc = jnp.split(x_dbl, [DT_RANK, DT_RANK + D_STATE], axis=-1)
            dt = jax.nn.softplus(jnp.einsum('blr,dr->bld', dt, dt_proj_w) + dt_proj_b)
            A = -jnp.exp(A_log)

            def step(h, inputs):
                dt_t, x_t, B_t, C_t = inputs
                h = h * jnp.exp(dt_t[..., None] * A) + (dt_t * x_t)[..., None] * B_t[:, None, :]
                y = jnp.einsum('bds,bs->bd', h, C_t)
                return (h, y)
            h0 = jnp.zeros((u.shape[0], D_INNER, D_STATE), u.dtype)
            _, ys = lax.scan(step, h0, (dt.transpose(1, 0, 2), xc.transpose(1, 0, 2), Bc.transpose(1, 0, 2), Cc.transpose(1, 0, 2)))
            y = ys.transpose(1, 0, 2) + xc * D
            y = y * jax.nn.silu(z)
            return jnp.einsum('bld,ed->ble', y, out_proj_w)
        b, c, h, w = x.shape
        res = x
        u = _pixel_unshuffle(x, R)
        hh, ww = (h // R, w // R)
        u = u.reshape(b, D_MODEL, hh * ww).transpose(0, 2, 1)
        u = _layernorm(u, ln_gamma, ln_beta)
        u = _mamba(u, in_proj_w, conv_w, conv_b, x_proj_w, dt_proj_w, dt_proj_b, A_log, D, out_proj_w)
        u = u.transpose(0, 2, 1).reshape(b, D_MODEL, hh, ww)
        out = _pixel_shuffle(u, R)
        return out + res

    def _gn(v, G=4, eps=1e-5):
        B_, C_, H_, W_ = v.shape
        g = v.reshape(B_, G, C_ // G, H_, W_)
        m = jnp.mean(g, axis=(2, 3, 4), keepdims=True)
        s = jnp.var(g, axis=(2, 3, 4), keepdims=True)
        return ((g - m) / jnp.sqrt(s + eps)).reshape(v.shape)

    def _ln_c(v, eps=1e-6):
        m = jnp.mean(v, axis=1, keepdims=True)
        s = jnp.var(v, axis=1, keepdims=True)
        return (v - m) / jnp.sqrt(s + eps)

    def _ln_t(v, eps=1e-5):
        m = jnp.mean(v, axis=-1, keepdims=True)
        s = jnp.var(v, axis=-1, keepdims=True)
        return (v - m) / jnp.sqrt(s + eps)

    def _to_tokens(v):
        B_, C_, H_, W_ = v.shape
        return v.reshape(B_, C_, H_ * W_).transpose(0, 2, 1)
    def _from_tokens(t, like):
        B_, C_, H_, W_ = like.shape
        return t.transpose(0, 2, 1).reshape(B_, C_, H_, W_)

    x = x + _L0_conv_ref(_gn(x), L0_conv_fc0_w, L0_conv_fc0_b, L0_conv_w_w, L0_conv_w_b, L0_conv_sp_w1, L0_conv_sp_w2, L0_conv_betas, L0_conv_fc1_w, L0_conv_fc1_b, L0_conv_fc2_w, L0_conv_fc2_b)
    x = x + _L1_conv_ref(_gn(x), L1_conv_ln_gamma, L1_conv_ln_beta, L1_conv_in_proj_w, L1_conv_conv_w, L1_conv_conv_b, L1_conv_x_proj_w, L1_conv_dt_proj_w, L1_conv_dt_proj_b, L1_conv_A_log, L1_conv_D, L1_conv_out_proj_w)
    return x


_drawn_inputs = setup_inputs


def setup_inputs(seed=0):
    import zlib

    import numpy as np

    out = dict(_drawn_inputs(seed))
    spreads = {'L0_conv_betas': (0.5, 0.6),
     'L1_conv_ln_gamma': (1.0, 0.6),
     'L1_conv_ln_beta': (0.0, 0.778),
     'L1_conv_D': (1.0, 0.6)}
    factors = {'L0_conv_fc0_w': 8.0,
     'L0_conv_fc0_b': 8.0,
     'L0_conv_w_w': 8.0,
     'L0_conv_w_b': 8.0,
     'L0_conv_sp_w1': 8.0,
     'L0_conv_sp_w2': 43.56,
     'L0_conv_fc1_w': 8.0,
     'L0_conv_fc1_b': 58.484,
     'L0_conv_fc2_w': 8.0,
     'L0_conv_fc2_b': 200.0,
     'L1_conv_conv_b': 27.08,
     'L1_conv_dt_proj_b': 8.0,
     'L1_conv_A_log': 8.0}
    for name, (base, spread) in spreads.items():
        noise = np.random.default_rng([zlib.crc32(name.encode()), seed]).standard_normal(out[name].shape)
        drawn = base * np.exp(spread * noise) if base else spread * noise
        out[name] = jnp.asarray(drawn.astype(out[name].dtype))
    for name, factor in factors.items():
        out[name] = (out[name] * factor).astype(out[name].dtype)
    return out
```

```python
import concourse.bass as bass
from concourse import mybir
from contextlib import ExitStack
import numpy as np

F32 = mybir.dt.float32
BF16 = mybir.dt.bfloat16
ALU = mybir.AluOpType
ACT = mybir.ActivationFunctionType
AX = mybir.AxisListType

BATCH = 8
G = 4
SC = 2
WID = 10
MODES = 12
H = 256
HALF = H // 2
NLAYER = 4
KX = 2 * MODES
KY = MODES
QUAD = 32
CH = G * 2 * WID
PIX = HALF * H
BLOCK = 512
CHUNK = 4096
NCHUNK = PIX // CHUNK
NPAIR = PIX // (2 * BLOCK)
XQ = 64
NXQ = H // XQ
HID = 128


def fno_stage(nc, ctx_nb, x, x1, grid, ident, gblk, gnsel, dfty, dftx, invy, invx,
              w0, wl, bl, betas_row, betas_free, wsp, w1f, b1t, w2f, b2t):
    NB = ctx_nb
    ctx = ExitStack()
    with ctx:
        def sb(name, shape, dt=F32):
            return ctx.enter_context(nc.sbuf_tensor(name, shape, dt))

        def sem(name):
            return ctx.enter_context(nc.semaphore(name))

        h = sb("h", [128, PIX])
        scratch = sb("scratch", [128, 2 * XQ * CH])
        Gs = sb("Gs", [128, 2, G * WID, 2 * KX])
        wmix = sb("wmix", [128, 2, WID, KY, WID])
        ident_s = sb("ident_s", [128, 128])
        dfty_s = sb("dfty_s", [128, 2, 2 * KX])
        dftx_s = sb("dftx_s", [128, 2, 2, 2 * KY])
        invy_s = sb("invy_s", [128, 2, H])
        invx_s = sb("invx_s", [128, H])
        gblk_s = sb("gblk_s", [128, 128])
        gnsel_s = sb("gnsel_s", [128, 2])
        w0_s = sb("w0_s", [128, 128])
        wl_s = sb("wl_s", [128, NLAYER, 128])
        wcur = sb("wcur", [128, 128])
        bl_s = sb("bl_s", [128, NLAYER])
        spb = sb("spb", [128, NLAYER])
        beta_r = sb("beta_r", [128, NLAYER])
        sp_r = sb("sp_r", [128, NLAYER])
        inv_r = sb("inv_r", [128, NLAYER + 1])
        beta_f = sb("beta_f", [128, G])
        sp_f = sb("sp_f", [128, G])
        inv_f = sb("inv_f", [128, G])
        b1_s = sb("b1_s", [128, G])
        b1sp = sb("b1sp", [128, G])
        b2_s = sb("b2_s", [128, 1])
        spt = sb("spt", [128, 4 * NLAYER])
        fr = sb("fr", [128, 3, WID, KY])
        oc = sb("oc", [128, WID, QUAD])
        osn = sb("osn", [128, WID, QUAD])
        stats = sb("stats", [128, 8, 6])
        mv = sb("mv", [128, 2])
        dev = sb("dev", [128, 2])
        gn = sb("gn", [128, 4])
        gnm = sb("gnm", [128, 2])
        PS = ctx.enter_context(nc.psum_tensor("PSF", [128, 8, BLOCK], F32))

        hT = [scratch[:, q * XQ * CH:(q + 1) * XQ * CH].rearrange("p (x c) -> p x c", c=CH) for q in range(2)]
        xc = [scratch[:, q * CHUNK:(q + 1) * CHUNK] for q in range(2)]
        tmp = scratch[:, 0:WID * KY * 2 * WID].rearrange("p (o k r i) -> p o k r i", o=WID, k=KY, r=2)
        tmp_flat = scratch[:, 0:WID * KY * 2 * WID].rearrange("p (m r) -> p m r", r=2 * WID)
        S = scratch[:, CHUNK:CHUNK + HALF * 2 * WID].rearrange("p (y c) -> p y c", c=2 * WID)
        zflat = Gs[:, :, :, :].rearrange("p a c k -> p (a c k)")
        z = [zflat[:, 1024 * i:1024 * (i + 1)] for i in range(3)]
        wflat = wmix[:, :, :, :, :].rearrange("p r o k i -> p (r o k i)")
        w1_s = wflat[:, 0:8 * HID].rearrange("p (g m) -> p g m", m=HID)
        w2_s = wflat[:, 8 * HID:8 * HID + 8 * QUAD].rearrange("p (g m) -> p g m", m=QUAD)

        def bank(j, n=1):
            return PS[:, j:j + n, :].rearrange("p a b -> p (a b)")

        PAIR = [0, 4, 6]
        FBANK = 3
        GBANK = 4
        IBANKS = [4, 5, 6, 7, 0]

        const_in = sem("const_in")
        setup_v = sem("setup_v")
        setup_a = sem("setup_a")
        dense_in = sem("dense_in")
        st_part = sem("st_part")
        st_sum = sem("st_sum")
        st_v = sem("st_v")
        st_sqrt = sem("st_sqrt")
        xc_in = [sem("xc_in0"), sem("xc_in1")]
        xc_norm = sem("xc_norm")
        fc0_mm = sem("fc0_mm")
        h_written = sem("h_written")
        w_cur = sem("w_cur")
        wmix_in = sem("wmix_in")
        tr_ready = sem("tr_ready")
        tr_used = sem("tr_used")
        y_done = sem("y_done")
        g_used = sem("g_used")
        f_ready = sem("f_ready")
        f_copied = sem("f_copied")
        mixv = sem("mixv")
        o_ready = sem("o_ready")
        i_ready = sem("i_ready")
        s_ready = sem("s_ready")
        e_ready = sem("e_ready")
        w12_in = sem("w12_in")
        w2_scaled = sem("w2_scaled")
        xr_in = [sem("xr_in0"), sem("xr_in1")]
        z_mm = sem("z_mm")
        z_act = sem("z_act")
        o_mm = sem("o_mm")
        x1_done = sem("x1_done")
        x1_out = sem("x1_out")

        CONSTS = [(ident_s, ident), (dfty_s, dfty), (dftx_s, dftx), (invy_s, invy), (invx_s, invx),
                  (gblk_s, gblk), (gnsel_s, gnsel), (w0_s, w0), (wl_s, wl), (bl_s, bl),
                  (beta_r, betas_row), (beta_f, betas_free), (b1_s, b1t), (b2_s, b2t)]
        x_dense = x.rearrange("b c (s f) -> b (c s) f", s=16)
        x_half = x.rearrange("b c (s f) -> b (c s) f", s=2)
        x1_half = x1.rearrange("b c (s f) -> b (c s) f", s=2)
        HPB = 5 * NPAIR
        START = 1
        block = ctx.enter_context(nc.Block())

        carrier = sem("carrier")

        def stand(eng):
            eng.sem_inc(carrier, 1)

        def full(t):
            return t[tuple([slice(None)] * len(t.shape))]

        @block.sync
        def _(sp):
            sp.sem_inc(x1_out, START)
            for t, src in CONSTS:
                sp.dma_start(full(t), src).then_inc(const_in, 16)
            sp.wait_ge(setup_v, 1)

            with sp.Fori(0, NB) as b:
                sp.wait_ge(x1_out, START + b * (NCHUNK * G * 16))
                sp.dma_start(xc[0], x_dense[b]).then_inc(dense_in, 16)
                sp.wait_ge(st_part, 2 * b + 1)
                for c in range(NCHUNK):
                    if c >= 2:
                        sp.wait_ge(fc0_mm, b * NPAIR + (c - 1) * 4)
                    for g in range(G):
                        sp.dma_start(xc[c % 2][QUAD * g:QUAD * g + 4, :],
                                     x_half[b, 4 * g:4 * g + 4, c * CHUNK:(c + 1) * CHUNK]).then_inc(xc_in[c % 2], 16)
                        sp.dma_start(xc[c % 2][QUAD * g + 4:QUAD * g + 8, :],
                                     grid[:, c * CHUNK:(c + 1) * CHUNK]).then_inc(xc_in[c % 2], 16)
                with sp.Fori(0, NLAYER) as l:
                    n = b * NLAYER + l
                    sp.wait_ge(o_ready, START + n)
                    stand(sp)
                    sp.wait_ge(o_mm, START + b * (PIX // BLOCK))
                    sp.dma_start(wflat, wsp[l]).then_inc(wmix_in, 16)
                sp.wait_ge(o_ready, START + (b + 1) * NLAYER)
                sp.dma_start(wflat[:, 0:8 * HID], w1f).then_inc(w12_in, 16)
                sp.dma_start(wflat[:, 8 * HID:8 * HID + 8 * QUAD], w2f).then_inc(w12_in, 16)
                sp.wait_ge(h_written, START + (b + 1) * HPB)
                for c in range(NCHUNK + 1):
                    if c < NCHUNK:
                        if c >= 2:
                            sp.wait_ge(x1_out, START + b * (NCHUNK * G * 16) + (c - 1) * G * 16)
                        for g in range(G):
                            sp.dma_start(xc[c % 2][QUAD * g:QUAD * g + 4, :],
                                         x_half[b, 4 * g:4 * g + 4, c * CHUNK:(c + 1) * CHUNK]).then_inc(xr_in[c % 2], 16)
                    if c >= 1:
                        sp.wait_ge(x1_done, START + b * (PIX // BLOCK) + c * (CHUNK // BLOCK))
                        for g in range(G):
                            sp.dma_start(x1_half[b, 4 * g:4 * g + 4, (c - 1) * CHUNK:c * CHUNK],
                                         xc[(c - 1) % 2][QUAD * g:QUAD * g + 4, :]).then_inc(x1_out, 16)
            sp.wait_ge(x1_out, START + NB * NCHUNK * G * 16)

        def pe_layer(pe, n, hbase):
            def transposes(q):
                for t in range(16 * q, 16 * q + 16):
                    if t >= 3:
                        pe.wait_ge(tr_used, n * 64 + t - 2)
                    for j in range(4):
                        xx = 4 * t + j
                        m = nc.tensor.transpose(bank(t % 3)[:, 128 * j:128 * j + 128],
                                                h[:, xx:xx + (HALF - 1) * H + 1:H], ident_s[:, :])
                    m.then_inc(tr_ready, 1)

            def rows(q):
                pe.wait_ge(tr_used, n * 64 + 16 * (q + 1))
                if q == 2:
                    pe.wait_ge(g_used, n * 8 + 4)
                for ch in range(G * WID):
                    g, c = ch // WID, ch % WID
                    for yh in range(2):
                        col = (ch % WID) * 2 * KX
                        m = nc.tensor.matmul(
                            PS[XQ * (q % 2):XQ * (q % 2) + XQ, GBANK + g, col:col + 2 * KX],
                            hT[q % 2][:, :, g * 2 * WID + yh * WID + c], dfty_s[:, yh, :],
                            start=(yh == 0), stop=(yh == 1), skip_group_check=True)
                m.then_inc(y_done, 1)

            pe.wait_ge(h_written, START + hbase)
            transposes(0)
            transposes(1)
            rows(0)
            transposes(2)
            rows(1)
            transposes(3)
            rows(2)
            rows(3)
            pe.wait_ge(g_used, n * 8 + 8)
            for c in range(WID):
                for k, (xh, ri) in enumerate([(0, 0), (0, 1), (1, 0), (1, 1)]):
                    for g in range(G):
                        m = nc.tensor.matmul(
                            PS[QUAD * g:QUAD * g + KX, FBANK, c * 2 * KY:(c + 1) * 2 * KY],
                            Gs[:, xh, g * WID + c, ri * KX:(ri + 1) * KX], dftx_s[:, xh, ri, :],
                            start=(k == 0), stop=(k == 3), skip_group_check=True,
                            tile_position=(0, QUAD * g))
            m.then_inc(f_ready, 1)
            pe.wait_ge(o_ready, START + n + 1)
            stand(pe)
            for o in range(WID):
                for g in range(G):
                    q = slice(QUAD * g, QUAD * g + KX)
                    out = PS[QUAD * g:QUAD * (g + 1), IBANKS[o // 2], (o % 2) * H:(o % 2 + 1) * H]
                    nc.tensor.matmul(out, oc[q, o, :], invy_s[q, 0, :], start=True, stop=False,
                                     skip_group_check=True, tile_position=(QUAD * g, QUAD * g))
                    m = nc.tensor.matmul(out, osn[q, o, :], invy_s[q, 1, :], start=False, stop=True,
                                         skip_group_check=True, tile_position=(QUAD * g, QUAD * g))
                if o % 2:
                    m.then_inc(i_ready, 1)
            pe.wait_ge(w_cur, n + 1)
            pe.wait_ge(s_ready, (n + 1) * 5)
            for k in range(NPAIR):
                if k >= 3:
                    pe.wait_ge(h_written, START + hbase + k - 2)
                for j in range(2):
                    blk = 2 * k + j
                    b0 = PAIR[k % 3] + j
                    nc.tensor.matmul(bank(b0), wcur[:, :], h[:, BLOCK * blk:BLOCK * (blk + 1)],
                                     start=True, stop=False, skip_group_check=True)
                    for r in range(2):
                        for g in range(G):
                            q = slice(QUAD * g, QUAD * g + 2 * KY)
                            m = nc.tensor.matmul(
                                PS[QUAD * g:QUAD * g + 2 * WID, b0, r * H:(r + 1) * H],
                                S[q, 2 * blk + r, :], invx_s[q, :], start=False, stop=True,
                                skip_group_check=True, tile_position=(QUAD * g, QUAD * g))
                m.then_inc(e_ready, 1)

        @block.tensor
        def _(pe):
            pe.sem_inc(o_mm, START)
            pe.wait_ge(const_in, 16 * len(CONSTS))
            pe.wait_ge(setup_v, 2)
            with pe.Fori(0, NB) as b:
                pe.wait_ge(x1_done, START + b * (PIX // BLOCK))
                pe.wait_ge(st_part, 2 * b + 1)
                nc.tensor.matmul(bank(0)[:, 0:1], gblk_s[:, :], mv[:, 0:1], start=True, stop=True).then_inc(st_sum, 1)
                pe.wait_ge(st_part, 2 * b + 2)
                nc.tensor.matmul(bank(0)[:, 1:2], gblk_s[:, :], dev[:, 1:2], start=True, stop=True).then_inc(st_sum, 1)
                pe.wait_ge(st_sqrt, b + 1)
                stand(pe)
                with pe.Fori(0, NCHUNK // 2) as cc:
                    for c in range(2):
                        pe.wait_ge(xc_norm, b * NCHUNK + cc * 2 + (c + 1))
                        for k in range(4):
                            if c == 0 and k < 3:
                                pe.wait_ge(h_written, START + b * HPB + cc * 8)
                            else:
                                pe.wait_ge(h_written, START + b * HPB + cc * 8 + (4 * c + k - 2))
                            p0 = PAIR[(4 * c + k) % 3]
                            for j in range(2):
                                m = nc.tensor.matmul(bank(p0 + j), w0_s[:, :],
                                                     xc[c][:, (2 * k + j) * BLOCK:(2 * k + j + 1) * BLOCK],
                                                     start=True, stop=True)
                            m.then_inc(fc0_mm, 1)
                with pe.Fori(0, NLAYER) as l:
                    pe_layer(pe, b * NLAYER + l, b * HPB + (l + 1) * NPAIR)
                pe.wait_ge(h_written, START + (b + 1) * HPB)
                pe.wait_ge(w2_scaled, b + 1)
                stand(pe)
                NBLK = PIX // BLOCK
                with pe.Fori(0, NBLK // 2) as kk:
                    for r in range(2):
                        for g in range(G):
                            i = r * G + g
                            zi = b * (NBLK * G) + kk * (2 * G) + i
                            if i >= 2:
                                pe.wait_ge(z_act, START + zi - 1)
                            else:
                                pe.wait_ge(z_act, START + b * (NBLK * G) + kk * (2 * G))
                            p0 = [0, 4][i % 2]
                            for yh in range(2):
                                m = nc.tensor.matmul(bank(p0 + yh), w1_s[:, 2 * g + yh, :],
                                                     h[:, bass.ds(kk * (2 * BLOCK) + r * BLOCK, BLOCK)],
                                                     start=True, stop=True)
                            m.then_inc(z_mm, 1)
                            if g == 0:
                                pe.wait_ge(x1_done, START + b * NBLK + kk * 2)
                            pe.wait_ge(z_act, START + zi + 1)
                            for yh in range(2):
                                m = nc.tensor.matmul(PS[QUAD * g:QUAD * (g + 1), 6 + r, :],
                                                     w2_s[:, 2 * g + yh, :],
                                                     z[i % 2][:, yh * BLOCK:(yh + 1) * BLOCK],
                                                     start=(yh == 0), stop=(yh == 1),
                                                     skip_group_check=True, tile_position=(0, QUAD * g))
                        m.then_inc(o_mm, 1)

        def act_layer(act, n, l, hbase, last):
            act.wait_ge(h_written, START + hbase)
            stand(act)
            nc.scalar.copy(wcur[:, :], wl_s[:, bass.ds(l, 1), :].rearrange("p a m -> p (a m)")).then_inc(w_cur, 1)
            for xh in range(2):
                act.wait_ge(y_done, n * 4 + 2 * xh + 2)
                for g in range(4):
                    nc.scalar.copy(
                        Gs[:, xh, g * WID:(g + 1) * WID, :].rearrange("p c k -> p (c k)"),
                        PS[:, GBANK + g, 0:WID * 2 * KX]).then_inc(g_used, 1)
            act.wait_ge(f_ready, n + 1)
            stand(act)
            fv = PS[:, FBANK, 0:WID * 2 * KY].rearrange("p (c r k) -> p r c k", r=2, k=KY)
            for part in range(2):
                nc.scalar.activation(fr[:, part, :, :], fv[:, part, :, :], ACT.Copy,
                                     scale=inv_r[:, bass.ds(l, 1)]).then_inc(f_copied, 1)
            for j in range(5):
                act.wait_ge(i_ready, n * 5 + j + 1)
                nc.scalar.copy(
                    S.rearrange("p y (h o) -> p o h y", h=2)[:, 2 * j, :, :],
                    PS[:, IBANKS[j], 0:H].rearrange("p (h y) -> p h y", h=2))
                nc.scalar.copy(
                    S.rearrange("p y (h o) -> p o h y", h=2)[:, 2 * j + 1, :, :],
                    PS[:, IBANKS[j], H:2 * H].rearrange("p (h y) -> p h y", h=2)).then_inc(s_ready, 1)
            for k in range(NPAIR):
                act.wait_ge(e_ready, n * NPAIR + k + 1)
                stand(act)
                out = h[:, 2 * BLOCK * k:2 * BLOCK * (k + 1)]
                if last:
                    nc.scalar.activation(out, bank(PAIR[k % 3], 2), ACT.Identity,
                                         bias=bl_s[:, NLAYER - 1:NLAYER]).then_inc(h_written, 1)
                else:
                    nc.scalar.activation(out, bank(PAIR[k % 3], 2), ACT.Silu, scale=sp_r[:, bass.ds(l, 1)],
                                         bias=spb[:, bass.ds(l, 1)]).then_inc(h_written, 1)

        @block.scalar
        def _(act):
            act.sem_inc(h_written, START)
            act.sem_inc(z_act, START)
            act.wait_ge(const_in, 16 * len(CONSTS))
            act.wait_ge(setup_v, 3)
            nc.scalar.activation(spt[:, 8:16], spt[:, 0:8], ACT.Exp, scale=-1.0).then_inc(setup_a, 1)
            act.wait_ge(setup_a, 1)
            nc.scalar.activation(spt[:, 8:16], spt[:, 8:16], ACT.Ln, bias=1.0).then_inc(setup_a, 1)
            act.wait_ge(setup_v, 9)
            with act.Fori(0, NB) as b:
                act.wait_ge(st_v, (b + 1) * 3)
                nc.scalar.activation(gn[:, 2:3], gn[:, 1:2], ACT.Sqrt).then_inc(st_sqrt, 1)
                with act.Fori(0, NPAIR // 8) as kk:
                    for k in range(8):
                        act.wait_ge(fc0_mm, b * NPAIR + kk * 8 + (k + 1))
                        stand(act)
                        nc.scalar.copy(h[:, bass.ds(kk * (16 * BLOCK) + k * 2 * BLOCK, 2 * BLOCK)],
                                       bank(PAIR[k % 3], 2)).then_inc(h_written, 1)
                with act.Fori(0, NLAYER - 1) as l:
                    act_layer(act, b * NLAYER + l, l, b * HPB + (l + 1) * NPAIR, False)
                act_layer(act, b * NLAYER + (NLAYER - 1), NLAYER - 1, b * HPB + NLAYER * NPAIR, True)
                NBLK = PIX // BLOCK
                with act.Fori(0, NBLK // 2) as kk:
                    for i in range(2 * G):
                        g = i % G
                        act.wait_ge(z_mm, b * (NBLK * G) + kk * (2 * G) + i + 1)
                        nc.scalar.activation(z[i % 2], bank([0, 4][i % 2], 2), ACT.Silu,
                                             scale=sp_f[:, g:g + 1], bias=b1sp[:, g:g + 1]).then_inc(z_act, 1)

        @block.vector
        def _(v):
            v.sem_inc(o_ready, START)
            v.sem_inc(x1_done, START)
            v.memset(scratch[:, :], 0.0).then_inc(setup_v, 1)
            v.memset(PS[:, FBANK, :], 0.0)
            v.memset(oc[:, :, :], 0.0)
            v.memset(osn[:, :, :], 0.0).then_inc(setup_v, 1)
            v.wait_ge(const_in, 16 * len(CONSTS))
            v.scalar_tensor_tensor(spt[:, 0:4], beta_r[:, :], -1.0, beta_r[:, :], ALU.mult, ALU.max)
            v.scalar_tensor_tensor(spt[:, 4:8], beta_f[:, :], -1.0, beta_f[:, :], ALU.mult, ALU.max).then_inc(setup_v, 1)
            v.wait_ge(setup_a, 2)
            v.scalar_tensor_tensor(sp_r[:, :], beta_r[:, :], 0.0, spt[:, 8:12], ALU.max, ALU.add).then_inc(setup_v, 1)
            v.scalar_tensor_tensor(sp_f[:, :], beta_f[:, :], 0.0, spt[:, 12:16], ALU.max, ALU.add).then_inc(setup_v, 1)
            v.wait_ge(setup_v, 5)
            v.tensor_scalar(sp_r[:, :], sp_r[:, :], 1e-30, None, ALU.max)
            v.tensor_scalar(sp_f[:, :], sp_f[:, :], 1e-30, None, ALU.max).then_inc(setup_v, 1)
            v.wait_ge(setup_v, 6)
            v.tensor_tensor(spb[:, :], sp_r[:, :], bl_s[:, :], ALU.mult)
            v.tensor_tensor(b1sp[:, :], sp_f[:, :], b1_s[:, :], ALU.mult)
            v.tensor_scalar(spt[:, 0:4], sp_r[:, :], 1.1, None, ALU.mult)
            v.tensor_scalar(spt[:, 4:8], sp_f[:, :], 1.1, None, ALU.mult).then_inc(setup_v, 1)
            v.wait_ge(setup_v, 7)
            v.memset(inv_r[:, 0:1], 1.0)
            v.reciprocal(inv_r[:, 1:1 + NLAYER], spt[:, 0:4])
            v.reciprocal(inv_f[:, :], spt[:, 4:8]).then_inc(setup_v, 1)
            v.wait_ge(setup_v, 8)
            for l in range(1, NLAYER):
                v.tensor_scalar(wl_s[:, l, :], wl_s[:, l, :], inv_r[:, l:l + 1], None, ALU.mult)
            v.memset(stats[:, :, :], 0.0).then_inc(setup_v, 1)
            v.wait_ge(setup_v, 9)
            with v.Fori(0, NB) as b:
                v.wait_ge(dense_in, (b + 1) * 16)
                for j in range(8):
                    m = v.bn_stats(stats[:, j, :], xc[0][:, j * 512:(j + 1) * 512])
                m.then_inc(st_v, 1)
                v.wait_ge(st_v, b * 3 + 1)
                stand(v)
                v.bn_aggr(mv[:, :], stats[:, :, :].rearrange("p a b -> p (a b)")).then_inc(st_part, 1)
                v.wait_ge(st_part, 2 * b + 1)
                v.wait_ge(st_sum, 2 * b + 1)
                v.tensor_copy(gn[:, 0:1], bank(0)[:, 0:1])
                v.tensor_tensor(dev[:, 0:1], mv[:, 0:1], bank(0)[:, 0:1], ALU.subtract).then_inc(st_v, 1)
                v.wait_ge(st_v, b * 3 + 2)
                v.scalar_tensor_tensor(dev[:, 1:2], dev[:, 0:1], dev[:, 0:1], mv[:, 1:2],
                                       ALU.mult, ALU.add).then_inc(st_part, 1)
                v.wait_ge(st_sum, 2 * b + 2)
                v.tensor_scalar(gn[:, 1:2], bank(0)[:, 1:2], 1e-5, None, ALU.add).then_inc(st_v, 1)
                v.wait_ge(st_sqrt, b + 1)
                v.reciprocal(gn[:, 3:4], gn[:, 2:3])
                v.tensor_scalar(gnm[:, 0:1], gn[:, 0:1], gnsel_s[:, 0:1], None, ALU.mult).then_inc(mixv, 1)
                v.wait_ge(mixv, (b * (2 + 8 * NLAYER)) + 1)
                v.tensor_scalar(gnm[:, 1:2], gn[:, 3:4], gnsel_s[:, 0:1], gnsel_s[:, 1:2],
                                ALU.mult, ALU.add).then_inc(mixv, 1)
                v.wait_ge(mixv, (b * (2 + 8 * NLAYER)) + 2)
                stand(v)
                with v.Fori(0, NCHUNK // 2) as cc:
                    for c in range(2):
                        v.wait_ge(xc_in[c], (b * (NCHUNK // 2) + cc + 1) * (2 * G * 16))
                        v.tensor_scalar(xc[c], xc[c], gnm[:, 0:1], gnm[:, 1:2], ALU.subtract,
                                        ALU.mult).then_inc(xc_norm, 1)
                with v.Fori(0, NLAYER) as l:
                    n = b * NLAYER + l
                    for t in range(64):
                        if t == 32 or t == 48:
                            v.wait_ge(y_done, n * 4 + (t // 16 - 1))
                        v.wait_ge(tr_ready, n * 64 + t + 1)
                        src = bank(t % 3).rearrange("p (x g r) -> p x g r", x=4, g=G)[:, :, :, 0:2 * WID]
                        x0 = 4 * (t % 16)
                        dst = hT[(t // 16) % 2][:, x0:x0 + 4, :].rearrange("p x (g r) -> p x g r", g=G)
                        v.tensor_copy(dst, src).then_inc(tr_used, 1)
                    v.wait_ge(f_copied, n * 2 + 2)
                    mv0 = b * (2 + 8 * NLAYER) + 2 + l * 8
                    v.tensor_scalar(fr[:, 2, :, :], fr[:, 1, :, :], -1.0, None, ALU.mult).then_inc(mixv, 1)
                    v.wait_ge(mixv, mv0 + 1)
                    v.wait_ge(wmix_in, (n + 1) * 16)

                    def product(slot, w_part, f_part):
                        f = fr[:, f_part, :, :].rearrange("p i k -> p k i")
                        f = f[:, None, :, :].to_broadcast([128, WID, KY, WID])
                        return v.tensor_tensor(tmp[:, :, :, slot, :], wmix[:, w_part, :, :, :], f, ALU.mult)

                    def gather(part):
                        return v.tensor_reduce(oc[:, :, part * KY:(part + 1) * KY],
                                               tmp_flat.rearrange("p (o k) r -> p o k r", o=WID),
                                               AX.X, ALU.add)
                    product(0, 0, 0)
                    product(1, 1, 2).then_inc(mixv, 1)
                    v.wait_ge(mixv, mv0 + 2)
                    gather(0).then_inc(mixv, 1)
                    v.wait_ge(mixv, mv0 + 3)
                    product(0, 0, 1)
                    product(1, 1, 0).then_inc(mixv, 1)
                    v.wait_ge(mixv, mv0 + 4)
                    gather(1).then_inc(mixv, 1)
                    v.wait_ge(mixv, mv0 + 5)
                    v.tensor_scalar(osn[:, :, 0:KY], oc[:, :, KY:2 * KY], -1.0, None, ALU.mult).then_inc(mixv, 1)
                    v.tensor_copy(osn[:, :, KY:2 * KY], oc[:, :, 0:KY]).then_inc(mixv, 1)
                    v.wait_ge(mixv, mv0 + 7)
                    v.nop().then_inc(o_ready, 1)
                    v.nop().then_inc(mixv, 1)
                v.wait_ge(w12_in, (b + 1) * 32)
                for g in range(G):
                    m = v.tensor_scalar(w2_s[:, 2 * g:2 * g + 2, :], w2_s[:, 2 * g:2 * g + 2, :],
                                        inv_f[:, g:g + 1], None, ALU.mult)
                m.then_inc(w2_scaled, 1)
                NBLK = PIX // BLOCK
                PER = CHUNK // BLOCK
                with v.Fori(0, NCHUNK // 2) as cc:
                    for c in range(2):
                        v.wait_ge(xr_in[c], (b * (NCHUNK // 2) + cc + 1) * (G * 16))
                        for k in range(PER):
                            v.wait_ge(o_mm, START + b * NBLK + cc * (2 * PER) + (c * PER + k + 1))
                            blk = xc[c][:, k * BLOCK:(k + 1) * BLOCK]
                            v.scalar_tensor_tensor(blk, bank(6 + k % 2), b2_s[:, 0:1], blk, ALU.add,
                                                   ALU.add).then_inc(x1_done, 1)


def fno_constants():
    f = np.float32
    c = {}
    kx = np.concatenate([np.arange(MODES), np.arange(H - MODES, H)])
    ky = np.arange(KY)
    y = np.arange(H)
    lin = np.linspace(0.0, 1.0, H).astype(f)
    grid = np.zeros((4, HALF, H), f)
    grid[0] = lin[:HALF, None]
    grid[1] = lin[HALF:, None]
    grid[2] = lin[None, :]
    grid[3] = 1.0
    c["grid"] = grid.reshape(4, PIX)
    c["ident"] = np.eye(128, dtype=f)
    c["gblk"] = (np.kron(np.eye(G), np.ones((QUAD, QUAD))) / QUAD).astype(f)
    sel = np.zeros((128, 2), f)
    for g in range(G):
        sel[QUAD * g:QUAD * g + 4, 0] = 1
        sel[QUAD * g + 4:QUAD * g + 8, 1] = 1
    c["gnsel"] = sel
    a = 2 * np.pi * (np.outer(y, kx) % H) / H
    c["dfty"] = np.concatenate([np.cos(a), -np.sin(a)], 1).reshape(2, HALF, 2 * KX).transpose(1, 0, 2).astype(f)
    a = 2 * np.pi * (np.outer(y, ky) % H) / H
    cs, sn = np.cos(a), np.sin(a)
    dx = np.stack([np.concatenate([cs, -sn], 1), np.concatenate([sn, cs], 1)], 1)
    c["dftx"] = dx.reshape(2, HALF, 2, 2 * KY).transpose(1, 0, 2, 3).astype(f)
    iy = np.zeros((G, QUAD, 2, H))
    a = 2 * np.pi * (np.outer(kx, y) % H) / H
    iy[:, :KX, 0] = np.cos(a)
    iy[:, :KX, 1] = np.sin(a)
    c["invy"] = iy.reshape(128, 2, H).astype(f)
    ix = np.zeros((G, QUAD, H))
    wt = np.where(ky == 0, 1.0, 2.0)[:, None] / (H * H)
    a = 2 * np.pi * (np.outer(ky, y) % H) / H
    ix[:, :KY] = wt * np.cos(a)
    ix[:, KY:2 * KY] = -wt * np.sin(a)
    c["invx"] = ix.reshape(128, H).astype(f)
    return {k: np.ascontiguousarray(v) for k, v in c.items()}


def fno_weights(fc0_w, fc0_b, w_w, w_b, sp_w1, sp_w2, betas, fc1_w, fc1_b, fc2_w, fc2_b):
    f = np.float32
    c = {}
    w0 = np.zeros((128, 128), f)
    wl = np.zeros((128, NLAYER, 128), f)
    bl = np.zeros((128, NLAYER), f)
    w1 = np.zeros((128, 8, HID), f)
    w2 = np.zeros((HID, 8, QUAD), f)
    b2 = np.zeros((128, 1), f)
    for g in range(G):
        for yh in range(2):
            cols = slice(QUAD * g + WID * yh, QUAD * g + WID * (yh + 1))
            for i in range(SC):
                w0[QUAD * g + 2 * i + yh, cols] = fc0_w[g, :, i]
                w2[:, 2 * g + yh, 2 * i + yh] = fc2_w[g, i]
                b2[QUAD * g + 2 * i + yh, 0] = fc2_b[SC * g + i]
            w0[QUAD * g + 4 + yh, cols] = fc0_w[g, :, SC]
            w0[QUAD * g + 6, cols] = fc0_w[g, :, SC + 1]
            w0[QUAD * g + 7, cols] = fc0_b[WID * g:WID * (g + 1)]
            wl[cols, :, cols] = w_w[:, g].transpose(2, 0, 1)
            bl[cols] = w_b[:, WID * g:WID * (g + 1)].T
            w1[cols, 2 * g + yh] = fc1_w[g].T
    c["w0"], c["wl"], c["bl"], c["w1f"], c["w2f"], c["b2t"] = w0, wl, bl, w1.reshape(128, -1), w2.reshape(128, -1), b2
    c["betas_row"] = np.repeat(betas.T, QUAD, axis=0)
    c["betas_free"] = np.broadcast_to(betas[NLAYER - 1], (128, G))
    c["b1t"] = fc1_b.reshape(G, HID).T
    sp = np.concatenate([sp_w1, sp_w2], axis=4)
    full = np.zeros((NLAYER, G, QUAD, 2, WID, KY, WID), f)
    full[:, :, :KX] = sp.transpose(0, 1, 4, 6, 3, 5, 2)
    c["wsp"] = full.reshape(NLAYER, 128, 2 * WID * KY * WID)
    return {k: np.ascontiguousarray(v) for k, v in c.items()}


R = 4
DM = 128
DI = 256
NS = 64
DTR = 8
KC = 4
L = (H // R) * (H // R)
TC = 1024
NTC = L // TC
RPC = TC * R // H * R
SB = 32
PIECES = 3
BK = 512


def mamba_stage(nc, NB, x1, out, ident, gblk, gmap, ones, sel, win, wx, wxd, wdt, convw, convb,
                dtb, alog, dmat, wout, lng, lnb):
    ctx = ExitStack()
    with ctx:
        def sb(name, shape, dt=F32):
            return ctx.enter_context(nc.sbuf_tensor(name, shape, dt))

        def sem(name):
            return ctx.enter_context(nc.semaphore(name))

        ident_m = sb("ident_m", [128, 128])
        gblk_m = sb("gblk_m", [128, 128])
        gmap_m = sb("gmap_m", [128, 128])
        ones_m = sb("ones_m", [128, 128])
        sel_m = sb("sel_m", [PIECES * SB, SB, 128], BF16)
        win_m = sb("win_m", [128, 4, 128])
        wx_m = sb("wx_m", [128, 2, 128])
        wxd_m = sb("wxd_m", [128, 2, DTR])
        wdt_m = sb("wdt_m", [DTR, 2, 128])
        convw_m = sb("convw_m", [128, 2, KC])
        convb_m = sb("convb_m", [128, 2])
        dtb_m = sb("dtb_m", [128, 2])
        a_log = sb("a_log", [128, SB, 4])
        a_neg = sb("a_neg", [128, SB, 4])
        dmat_m = sb("dmat_m", [128, 2, 128])
        wout_m = sb("wout_m", [128, 2, 128])
        lng_m = sb("lng_m", [128, 1])
        lnb_m = sb("lnb_m", [128, 1])
        eps = sb("eps", [128, 1])
        zero16 = sb("zero16", [1, BK], BF16)
        shuf = sb("shuf", [128, R * TC])
        u = sb("u", [128, TC])
        xg = sb("xg", [128, TC])
        xres = sb("xres", [128, TC])
        cen = sb("cen", [128, TC])
        sq = sb("sq", [128, TC])
        fin = sb("fin", [128, TC])
        xpad = sb("xpad", [128, 2, KC - 1 + TC])
        ta = sb("ta", [128, 2, TC])
        tb = sb("tb", [128, 2, TC])
        xs = sb("xs", [128, 2, TC])
        sz = sb("sz", [128, 2, TC])
        dt_ = sb("dt_", [128, 2, TC])
        dtx = sb("dtx", [128, 2, TC])
        dtl = sb("dtl", [DTR, TC])
        pieces = sb("pieces", [128, PIECES, TC], BF16)
        bcp = sb("bcp", [PIECES * SB, 4, TC], BF16)
        decay = sb("decay", [128, 4, TC])
        drive = sb("drive", [128, 4, TC])
        hs = sb("hs", [128, 4, TC])
        hc = sb("hc", [128, 4, TC])
        cb = sb("cb", [128, 2, TC])
        carry = sb("carry", [128, SB, 4])
        stats = sb("stats_m", [128, 8, 6])
        mv = sb("mv_m", [128, 2])
        dev = sb("dev_m", [128, 2])
        gn = sb("gn_m", [128, 4])
        PS = ctx.enter_context(nc.psum_tensor("PSM", [128, 8, BK], F32))

        def bank(j, n=2):
            return PS[:, j:j + n, :].rearrange("p a b -> p (a b)")

        xa, xd, fo, oi = (shuf[QUAD * i:QUAD * (i + 1), :] for i in range(4))

        sel_in_f32 = shuf[0:PIECES * SB, :]
        CONSTS = [(ident_m, ident), (gblk_m, gblk), (gmap_m, gmap), (ones_m, ones), (sel_in_f32, sel),
                  (win_m, win), (wx_m, wx), (wxd_m, wxd), (wdt_m, wdt), (convw_m, convw),
                  (convb_m, convb), (dtb_m, dtb), (a_log, alog), (dmat_m, dmat), (wout_m, wout),
                  (lng_m, lng), (lnb_m, lnb)]
        const_in = sem("mconst_in")
        setup_v = sem("msetup_v")
        setup_a = sem("msetup_a")
        dense_in = sem("mdense_in")
        bn_done = sem("bn_done")
        st_part = sem("mst_part")
        st_sum = sem("mst_sum")
        dev_done = sem("dev_done")
        var_ready = sem("var_ready")
        st_sqrt = sem("mst_sqrt")
        gn_ready = sem("gn_ready")
        xa_in = sem("xa_in")
        deint = sem("deint")
        u_in = sem("u_in")
        xg_ready = sem("xg_ready")
        xres_ready = sem("xres_ready")
        mean_ready = sem("mean_ready")
        cen_ready = sem("cen_ready")
        sq_ready = sem("sq_ready")
        lnvar_ready = sem("lnvar_ready")
        std_ready = sem("std_ready")
        rstd_ready = sem("rstd_ready")
        un_half = sem("un_half")
        un_ready = sem("un_ready")
        xz_ready = sem("xz_ready")
        pad_front = sem("pad_front")
        xpad_ready = sem("xpad_ready")
        sz_ready = sem("sz_ready")
        tap = sem("tap")
        xs_ready = sem("xs_ready")
        bc_psum = sem("bc_psum")
        dtl_psum = sem("dtl_psum")
        dtl_ready = sem("dtl_ready")
        split = sem("split")
        bcp_in = sem("bcp_in")
        dt_psum = sem("dt_psum")
        v_ready = sem("v_ready")
        abs_ready = sem("abs_ready")
        e_ready = sem("me_ready")
        ln_ready = sem("ln_ready")
        spstep = sem("spstep")
        dtx_ready = sem("dtx_ready")
        y_open = sem("y_open")
        b_ready = sem("b_ready")
        c_ready = sem("c_ready")
        c_copied = sem("c_copied")
        bx_done = sem("bx_done")
        a_ready = sem("a_ready")
        scan_done = sem("scan_done")
        hc_done = sem("hc_done")
        red_done = sem("red_done")
        carried = sem("carried")
        y_ready = sem("y_ready")
        gated = sem("gated")
        o_psum = sem("o_psum")
        fin_ready = sem("fin_ready")
        fo_in = sem("fo_in")
        il_done = sem("il_done")
        out_done = sem("out_done")

        x_dense = x1.rearrange("b c (s f) -> b (c s) f", s=16)
        def image_rows(t, b, c):
            return t.rearrange("b c (n h r w) -> b n c r h w", n=NTC, r=R, w=H)[b, c]
        HH = TC * R // H
        AHEAD = 4

        START = 1
        block = ctx.enter_context(nc.Block())

        carrier = sem("mcarrier")

        def stand(eng):
            eng.sem_inc(carrier, 1)

        def full(t):
            return t[tuple([slice(None)] * len(t.shape))]

        @block.sync
        def _(sp):
            sp.sem_inc(out_done, START)
            sp.sem_inc(u_in, START)
            sp.sem_inc(fo_in, START)
            for t, src in CONSTS:
                sp.dma_start(full(t), src).then_inc(const_in, 16)
            sp.wait_ge(setup_v, 1)
            with sp.Fori(0, NB) as b:
                sp.wait_ge(out_done, START + b * (NTC * 16 * 8))
                sp.dma_start(shuf[:, :], x_dense[b]).then_inc(dense_in, 16)
                sp.wait_ge(bn_done, b + 1)
                stand(sp)
                with sp.Fori(0, NTC) as c:
                    k = b * NTC + c
                    sp.wait_ge(deint, START + k)
                    src = image_rows(x1, b, c)
                    for ch in range(8):
                        sp.dma_start(xa[R * ch:R * (ch + 1), :].rearrange("p (h w) -> p h w", w=H),
                                     src[ch]).then_inc(xa_in, 16)
                    sp.wait_ge(deint, START + k + 1)
                    for r in range(R):
                        sp.dma_start(u[QUAD * r:QUAD * (r + 1), :], xd[:, r * TC:(r + 1) * TC]).then_inc(u_in, 16)
                    sp.wait_ge(split, (k + 1) * 4)
                    for j in range(4):
                        for p in range(PIECES):
                            sp.dma_start(bcp[SB * p:SB * (p + 1), j, :],
                                         pieces[SB * j:SB * (j + 1), p, :]).then_inc(bcp_in, 16)
                    sp.wait_ge(fin_ready, k + 1)
                    for r in range(R):
                        sp.dma_start(fo[:, r * TC:(r + 1) * TC], fin[QUAD * r:QUAD * (r + 1), :]).then_inc(fo_in, 16)
                    sp.wait_ge(il_done, k + 1)
                    dst = image_rows(out, b, c)
                    for ch in range(8):
                        sp.dma_start(dst[ch],
                                     oi[R * ch:R * (ch + 1), :].rearrange("p (h w) -> p h w", w=H)).then_inc(out_done, 16)
            sp.wait_ge(out_done, START + NB * NTC * 16 * 8)

        @block.tensor
        def _(pe):
            def broadcast(k, r, jb):
                q = k * SB + r
                pe.wait_ge(bx_done, START + q * 4 + 2 * jb)
                for j in range(2):
                    m = nc.tensor.matmul(PS[:, 4 + j, :], sel_m[:, bass.ds(r, 1), :].rearrange("p a m -> p (a m)"),
                                         bcp[:, jb, j * BK:(j + 1) * BK], start=True, stop=True)
                m.then_inc(b_ready, 1)
                pe.wait_ge(c_copied, START + q * 2 + jb)
                for j in range(2):
                    m = nc.tensor.matmul(PS[:, 6 + j, :], sel_m[:, bass.ds(r, 1), :].rearrange("p a m -> p (a m)"),
                                         bcp[:, 2 + jb, j * BK:(j + 1) * BK], start=True, stop=True)
                m.then_inc(c_ready, 1)

            def reduce(k, r, jb):
                q = k * SB + r
                for dh in range(2):
                    pe.wait_ge(hc_done, q * 4 + (2 * jb + dh + 1 + AHEAD))
                    for j in range(2):
                        m = nc.tensor.matmul(PS[:, 2 * dh + j, :], ident_m[:, :],
                                             hc[:, 2 * jb + dh, j * BK:(j + 1) * BK],
                                             start=False, stop=False, skip_group_check=True)
                    m.then_inc(red_done, 1)

            pe.wait_ge(const_in, 16 * len(CONSTS))
            pe.wait_ge(setup_v, 1)
            pe.sem_inc(red_done, AHEAD)
            with pe.Fori(0, NB) as b:
                pe.wait_ge(st_part, 2 * b + 1)
                nc.tensor.matmul(PS[:, 0, 0:1], gblk_m[:, :], mv[:, 0:1], start=True, stop=True)
                nc.tensor.matmul(PS[:, 0, 2:3], gmap_m[:, :], mv[:, 0:1], start=True, stop=True).then_inc(st_sum, 1)
                pe.wait_ge(st_part, 2 * b + 2)
                nc.tensor.matmul(PS[:, 0, 4:5], gmap_m[:, :], dev[:, 1:2], start=True, stop=True).then_inc(st_sum, 1)
                with pe.Fori(0, NTC) as c:
                    k = b * NTC + c
                    pe.wait_ge(gn_ready, b + 1)
                    pe.wait_ge(xg_ready, k + 1)
                    for j in range(2):
                        m = nc.tensor.matmul(PS[:, j, :], ones_m[:, :], xg[:, j * BK:(j + 1) * BK], start=True, stop=True)
                    m.then_inc(mean_ready, 1)
                    pe.wait_ge(sq_ready, k + 1)
                    for j in range(2):
                        m = nc.tensor.matmul(PS[:, 2 + j, :], ones_m[:, :], sq[:, j * BK:(j + 1) * BK], start=True, stop=True)
                    m.then_inc(lnvar_ready, 1)
                    pe.wait_ge(un_ready, k + 1)
                    for mm in range(4):
                        for j in range(2):
                            m = nc.tensor.matmul(PS[:, 2 * mm + j, :], win_m[:, mm, :], cen[:, j * BK:(j + 1) * BK],
                                                 start=True, stop=True)
                    m.then_inc(xz_ready, 1)
                    pe.wait_ge(xs_ready, (k + 1) * 2)
                    pe.wait_ge(sz_ready, k + 1)
                    for j in range(2):
                        for dh in range(2):
                            m = nc.tensor.matmul(PS[:, j, :], wx_m[:, dh, :], xs[:, dh, j * BK:(j + 1) * BK],
                                                 start=(dh == 0), stop=(dh == 1))
                    m.then_inc(bc_psum, 1)
                    for j in range(2):
                        for dh in range(2):
                            m = nc.tensor.matmul(PS[0:DTR, 2 + j, :], wxd_m[:, dh, :], xs[:, dh, j * BK:(j + 1) * BK],
                                                 start=(dh == 0), stop=(dh == 1))
                    m.then_inc(dtl_psum, 1)
                    pe.wait_ge(dtl_ready, k + 1)
                    for dh in range(2):
                        for j in range(2):
                            m = nc.tensor.matmul(PS[:, 4 + 2 * dh + j, :], wdt_m[:, dh, :], dtl[:, j * BK:(j + 1) * BK],
                                                 start=True, stop=True)
                    m.then_inc(dt_psum, 1)
                    pe.wait_ge(split, (k + 1) * 4)
                    pe.wait_ge(v_ready, k + 1)
                    for j in range(4):
                        nc.tensor.matmul(PS[:, j, :], zero16[:, 0:128], zero16[:, :], start=True, stop=False,
                                         skip_group_check=True)
                    pe.wait_ge(bcp_in, (k + 1) * (12 * 16))
                    broadcast(k, 0, 0)
                    with pe.Fori(0, SB - 1) as r:
                        broadcast(k, r, 1)
                        reduce(k, r, 0)
                        broadcast(k, r + 1, 0)
                        reduce(k, r, 1)
                    broadcast(k, SB - 1, 1)
                    reduce(k, SB - 1, 0)
                    reduce(k, SB - 1, 1)
                    for dh in range(2):
                        for j in range(2):
                            m = nc.tensor.matmul(PS[:, 2 * dh + j, :], dmat_m[:, dh, :], xs[:, dh, j * BK:(j + 1) * BK],
                                                 start=False, stop=True, skip_group_check=True)
                    m.then_inc(y_ready, 1)
                    pe.wait_ge(gated, (k + 1) * 2)
                    for j in range(2):
                        for dh in range(2):
                            m = nc.tensor.matmul(PS[:, 4 + j, :], wout_m[:, dh, :], ta[:, dh, j * BK:(j + 1) * BK],
                                                 start=(dh == 0), stop=(dh == 1))
                    m.then_inc(o_psum, 1)

        @block.scalar
        def _(act):
            act.sem_inc(c_copied, START)
            def exps(k, r, jb):
                q = k * SB + r
                for dh in range(2):
                    i = 2 * jb + dh
                    act.wait_ge(scan_done, q * 4 + (i + 1))
                    stand(act)
                    nc.scalar.activation(decay[:, i, :], dt_[:, dh, :], ACT.Exp,
                                         scale=a_neg[:, bass.ds(r, 1), i:i + 1].rearrange("p a b -> p (a b)")).then_inc(a_ready, 1)
                act.wait_ge(c_ready, q * 2 + (jb + 1))
                act.wait_ge(hc_done, q * 4 + (2 * jb + 2))
                nc.scalar.copy(cb[:, jb, :], bank(6)).then_inc(c_copied, 1)

            def carry_out(k, r, jb):
                q = k * SB + r
                act.wait_ge(scan_done, q * 4 + (2 * jb + 2 + AHEAD))
                stand(act)
                nc.scalar.copy(carry[:, bass.ds(r, 1), 2 * jb:2 * jb + 2].rearrange("p a b -> p (a b)"),
                               hs[:, 2 * jb:2 * jb + 2, TC - 1:TC].rearrange("p a b -> p (a b)")).then_inc(carried, 1)

            act.sem_inc(carried, 2)
            act.wait_ge(const_in, 16 * len(CONSTS))
            nc.scalar.activation(a_neg[:, :, :], a_log[:, :, :], ACT.Exp).then_inc(setup_a, 1)
            act.wait_ge(setup_v, 2)
            with act.Fori(0, NB) as b:
                act.wait_ge(var_ready, b + 1)
                nc.scalar.activation(gn[:, 2:3], gn[:, 1:2], ACT.Sqrt).then_inc(st_sqrt, 1)
                with act.Fori(0, NTC) as c:
                    k = b * NTC + c
                    act.wait_ge(cen_ready, k + 1)
                    nc.scalar.activation(sq[:, :], cen[:, :], ACT.Square).then_inc(sq_ready, 1)
                    act.wait_ge(lnvar_ready, k + 1)
                    nc.scalar.activation(sq[:, :], bank(2), ACT.Sqrt, bias=eps[:, 0:1]).then_inc(std_ready, 1)
                    act.wait_ge(xz_ready, k + 1)
                    nc.scalar.copy(xpad[:, :, 0:KC - 1], xpad[:, :, TC:TC + KC - 1]).then_inc(pad_front, 1)
                    act.wait_ge(pad_front, k + 1)
                    nc.scalar.copy(xpad[:, :, KC - 1:], PS[:, 0:4, :].rearrange("p (d j) b -> p d (j b)", d=2)).then_inc(xpad_ready, 1)
                    nc.scalar.activation(sz[:, :, :].rearrange("p d t -> p (d t)"), bank(4, 4), ACT.Silu).then_inc(sz_ready, 1)
                    for dh in range(2):
                        act.wait_ge(tap, k * 8 + 7 + dh)
                        nc.scalar.activation(xs[:, dh, :], ta[:, dh, :], ACT.Silu, bias=convb_m[:, dh:dh + 1]).then_inc(xs_ready, 1)
                    act.wait_ge(dtl_psum, k + 1)
                    nc.scalar.copy(dtl[:, :], PS[0:DTR, 2:4, :].rearrange("p a b -> p (a b)")).then_inc(dtl_ready, 1)
                    act.wait_ge(dt_psum, k + 1)
                    nc.scalar.activation(ta[:, 0, :], bank(4), ACT.Identity, bias=dtb_m[:, 0:1])
                    nc.scalar.activation(ta[:, 1, :], bank(6), ACT.Identity, bias=dtb_m[:, 1:2]).then_inc(v_ready, 1)
                    act.wait_ge(abs_ready, k + 1)
                    nc.scalar.activation(tb[:, :, :], tb[:, :, :], ACT.Exp, scale=-1.0).then_inc(e_ready, 1)
                    act.wait_ge(e_ready, k + 1)
                    nc.scalar.activation(dt_[:, :, :], tb[:, :, :], ACT.Ln, bias=1.0).then_inc(ln_ready, 1)
                    act.wait_ge(spstep, (k + 1) * 4)
                    exps(k, 0, 0)
                    with act.Fori(0, SB - 1) as r:
                        exps(k, r, 1)
                        carry_out(k, r, 0)
                        exps(k, r + 1, 0)
                        carry_out(k, r, 1)
                    exps(k, SB - 1, 1)
                    carry_out(k, SB - 1, 0)
                    carry_out(k, SB - 1, 1)
                    act.wait_ge(fo_in, START + (k + 1) * 64)
                    act.wait_ge(out_done, START + k * (16 * 8))
                    nc.scalar.copy(oi.rearrange("p (t r) -> p r t", r=R),
                                   fo.rearrange("p (r t) -> p r t", r=R)).then_inc(il_done, 1)

        @block.gpsimd
        def _(pool):
            pool.sem_inc(deint, START)
            pool.sem_inc(hc_done, AHEAD)
            with pool.Fori(0, NB) as b:
                with pool.Fori(0, NTC) as c:
                    k = b * NTC + c
                    pool.wait_ge(xa_in, (k + 1) * (16 * 8))
                    pool.wait_ge(u_in, START + k * 64)
                    stand(pool)
                    nc.gpsimd.tensor_copy(xd.rearrange("p (r t) -> p r t", r=R),
                                          xa.rearrange("p (t r) -> p r t", r=R)).then_inc(deint, 1)
                    with pool.Fori(0, SB) as r:
                        q = k * SB + r
                        for jb in range(2):
                            for dh in range(2):
                                i = 2 * jb + dh
                                pool.wait_ge(scan_done, q * 4 + (i + 1 + AHEAD))
                                if dh == 0:
                                    pool.wait_ge(c_copied, START + q * 2 + (jb + 1))
                                pool.wait_ge(red_done, q * 4 + (i + 1))
                                nc.gpsimd.tensor_tensor(hc[:, i, :], hs[:, i, :], cb[:, jb, :], ALU.mult).then_inc(hc_done, 1)

        @block.vector
        def _(v):
            v.sem_inc(bx_done, START)
            v.memset(zero16[:, :], 0.0)
            v.wait_ge(const_in, 16 * len(CONSTS))
            v.tensor_copy(sel_m[:, :, :].rearrange("p r m -> p (r m)"), sel_in_f32).then_inc(setup_v, 1)
            v.memset(eps[:, :], 1e-5)
            v.wait_ge(setup_a, 1)
            v.tensor_scalar(a_neg[:, :, :], a_neg[:, :, :], -1.0, None, ALU.mult).then_inc(setup_v, 1)
            v.sem_inc(scan_done, AHEAD)
            with v.Fori(0, NB) as b:
                v.wait_ge(dense_in, (b + 1) * 16)
                for j in range(8):
                    m = v.bn_stats(stats[:, j, :], shuf[:, j * 512:(j + 1) * 512])
                m.then_inc(bn_done, 1)
                v.wait_ge(bn_done, b + 1)
                stand(v)
                v.bn_aggr(mv[:, :], stats[:, :, :].rearrange("p a b -> p (a b)")).then_inc(st_part, 1)
                v.wait_ge(carried, b * (NTC * SB * 2) + 2)
                v.memset(carry[:, :, :], 0.0)
                v.memset(xpad[:, :, TC:TC + KC - 1], 0.0)
                v.wait_ge(st_part, 2 * b + 1)
                v.wait_ge(st_sum, 2 * b + 1)
                v.tensor_tensor(dev[:, 0:1], mv[:, 0:1], PS[:, 0, 0:1], ALU.subtract).then_inc(dev_done, 1)
                v.tensor_copy(gn[:, 0:1], PS[:, 0, 2:3])
                v.wait_ge(dev_done, b + 1)
                v.scalar_tensor_tensor(dev[:, 1:2], dev[:, 0:1], dev[:, 0:1], mv[:, 1:2],
                                       ALU.mult, ALU.add).then_inc(st_part, 1)
                v.wait_ge(st_sum, 2 * b + 2)
                v.tensor_scalar(gn[:, 1:2], PS[:, 0, 4:5], 1e-5, None, ALU.add).then_inc(var_ready, 1)
                v.wait_ge(st_sqrt, b + 1)
                v.reciprocal(gn[:, 3:4], gn[:, 2:3]).then_inc(gn_ready, 1)
                v.wait_ge(gn_ready, b + 1)
                stand(v)
                with v.Fori(0, NTC) as c:
                    k = b * NTC + c
                    v.wait_ge(u_in, START + (k + 1) * 64)
                    v.tensor_scalar(xg[:, :], u[:, :], gn[:, 0:1], gn[:, 3:4], ALU.subtract, ALU.mult).then_inc(xg_ready, 1)
                    v.wait_ge(xg_ready, k + 1)
                    v.tensor_tensor(xres[:, :], xg[:, :], u[:, :], ALU.add).then_inc(xres_ready, 1)
                    v.wait_ge(mean_ready, k + 1)
                    v.tensor_tensor(cen[:, :], xg[:, :], bank(0), ALU.subtract).then_inc(cen_ready, 1)
                    v.wait_ge(std_ready, k + 1)
                    v.reciprocal(sq[:, :], sq[:, :]).then_inc(rstd_ready, 1)
                    v.wait_ge(rstd_ready, k + 1)
                    v.scalar_tensor_tensor(cen[:, :], cen[:, :], lng_m[:, 0:1], sq[:, :], ALU.mult, ALU.mult).then_inc(un_half, 1)
                    v.wait_ge(un_half, k + 1)
                    v.tensor_scalar(cen[:, :], cen[:, :], lnb_m[:, 0:1], None, ALU.add).then_inc(un_ready, 1)
                    v.wait_ge(xpad_ready, k + 1)
                    for t in range(KC):
                        for dh in range(2):
                            src = xpad[:, dh, t:t + TC]
                            w = convw_m[:, dh, t:t + 1]
                            if t == 0:
                                v.tensor_scalar(ta[:, dh, :], src, w, None, ALU.mult).then_inc(tap, 1)
                            else:
                                v.wait_ge(tap, k * 8 + 2 * t - 1 + dh)
                                v.scalar_tensor_tensor(ta[:, dh, :], src, w, ta[:, dh, :], ALU.mult, ALU.add).then_inc(tap, 1)
                    v.wait_ge(bc_psum, k + 1)
                    v.wait_ge(xs_ready, (k + 1) * 2)
                    v.tensor_copy(pieces[:, 0, :], bank(0)).then_inc(split, 1)
                    v.wait_ge(split, k * 4 + 1)
                    v.tensor_tensor(tb[:, 0, :], bank(0), pieces[:, 0, :], ALU.subtract).then_inc(split, 1)
                    v.wait_ge(split, k * 4 + 2)
                    v.tensor_copy(pieces[:, 1, :], tb[:, 0, :]).then_inc(split, 1)
                    v.wait_ge(split, k * 4 + 3)
                    v.tensor_tensor(pieces[:, 2, :], tb[:, 0, :], pieces[:, 1, :], ALU.subtract).then_inc(split, 1)
                    v.wait_ge(v_ready, k + 1)
                    v.wait_ge(split, k * 4 + 4)
                    v.scalar_tensor_tensor(tb[:, :, :], ta[:, :, :], -1.0, ta[:, :, :], ALU.mult, ALU.max).then_inc(abs_ready, 1)
                    v.wait_ge(ln_ready, k + 1)
                    v.tensor_scalar(dtx[:, :, :], tb[:, :, :], 1.0, 1.0, ALU.add, ALU.subtract).then_inc(spstep, 1)
                    v.scalar_tensor_tensor(dt_[:, :, :], ta[:, :, :], 0.0, dt_[:, :, :], ALU.max, ALU.add).then_inc(spstep, 1)
                    v.wait_ge(spstep, k * 4 + 1)
                    v.tensor_tensor(tb[:, :, :], tb[:, :, :], dtx[:, :, :], ALU.subtract).then_inc(spstep, 1)
                    v.wait_ge(spstep, k * 4 + 3)
                    v.tensor_tensor(dt_[:, :, :], dt_[:, :, :], tb[:, :, :], ALU.add).then_inc(spstep, 1)
                    v.wait_ge(spstep, k * 4 + 4)
                    v.tensor_tensor(dtx[:, :, :], dt_[:, :, :], xs[:, :, :], ALU.mult).then_inc(dtx_ready, 1)
                    v.wait_ge(dtx_ready, k + 1)
                    stand(v)
                    with v.Fori(0, SB) as r:
                        q = k * SB + r
                        for jb in range(2):
                            v.wait_ge(b_ready, q * 2 + (jb + 1))
                            for dh in range(2):
                                v.tensor_tensor(drive[:, 2 * jb + dh, :], dtx[:, dh, :], bank(4), ALU.mult).then_inc(bx_done, 1)
                            for dh in range(2):
                                i = 2 * jb + dh
                                v.wait_ge(bx_done, START + q * 4 + (i + 1))
                                v.wait_ge(a_ready, q * 4 + (i + 1))
                                v.wait_ge(hc_done, q * 4 + (i + 1))
                                v.wait_ge(carried, q * 2 + (jb + 1))
                                v.tensor_tensor_scan(hs[:, i, :], decay[:, i, :], drive[:, i, :],
                                                     carry[:, bass.ds(r, 1), i:i + 1].rearrange("p a b -> p (a b)"),
                                                     ALU.mult, ALU.add).then_inc(scan_done, 1)
                    v.wait_ge(y_ready, k + 1)
                    for dh in range(2):
                        v.tensor_tensor(ta[:, dh, :], sz[:, dh, :], bank(2 * dh), ALU.mult).then_inc(gated, 1)
                    v.wait_ge(o_psum, k + 1)
                    v.wait_ge(fo_in, START + k * 64)
                    v.tensor_tensor(fin[:, :], xres[:, :], bank(4), ALU.add).then_inc(fin_ready, 1)


def mamba_constants():
    f = np.float32
    c = {}
    c["ones"] = np.full((128, 128), 1.0 / DM, f)
    gp = np.repeat(np.arange(G), 32)
    gu = np.tile(np.repeat(np.arange(G), 8), R)
    c["gmap"] = ((gp[:, None] == gu[None, :]) / 32.0).astype(f)
    sel = np.zeros((PIECES, SB, SB, 128), f)
    for r in range(SB):
        sel[:, r, r, :] = 1
    c["sel"] = sel.reshape(PIECES * SB, SB * 128)
    return {k: np.ascontiguousarray(v) for k, v in c.items()}


def mamba_weights(ln_gamma, ln_beta, in_proj_w, conv_w, conv_b, x_proj_w, dt_proj_w, dt_proj_b, A_log, D, out_proj_w):
    f = np.float32
    c = {}
    perm = np.arange(DM).reshape(8, R, R).transpose(2, 0, 1).reshape(-1)
    c["win"] = in_proj_w[:, perm].T.reshape(DM, 4, 128)
    c["wx"] = x_proj_w[DTR:].T.reshape(2, 128, 128).transpose(1, 0, 2)
    c["wxd"] = x_proj_w[:DTR].T.reshape(2, 128, DTR).transpose(1, 0, 2)
    c["wdt"] = dt_proj_w.T.reshape(DTR, 2, 128)
    c["convw"] = conv_w.reshape(2, 128, KC).transpose(1, 0, 2)
    c["convb"] = conv_b.reshape(2, 128).T
    c["dtb"] = dt_proj_b.reshape(2, 128).T
    c["alog"] = A_log.reshape(2, 128, 2, SB).transpose(1, 3, 2, 0).reshape(128, SB, 4)
    dm = np.zeros((128, 2, 128), f)
    for dh in range(2):
        dm[np.arange(128), dh, np.arange(128)] = D[128 * dh:128 * (dh + 1)]
    c["dmat"] = dm
    c["wout"] = out_proj_w[perm].T.reshape(2, 128, 128).transpose(1, 0, 2)
    c["lng"] = ln_gamma[perm][:, None]
    c["lnb"] = ln_beta[perm][:, None]
    return {k: np.ascontiguousarray(v) for k, v in c.items()}


_FNO = "fc0_w fc0_b w_w w_b sp_w1 sp_w2 betas fc1_w fc1_b fc2_w fc2_b".split()
_MAMBA = "ln_gamma ln_beta in_proj_w conv_w conv_b x_proj_w dt_proj_w dt_proj_b A_log D out_proj_w".split()
_FNO_ARGS = "grid ident gblk gnsel dfty dftx invy invx w0 wl bl betas_row betas_free wsp w1f b1t w2f b2t".split()
_MAMBA_ARGS = "ident gblk gmap ones sel win wx wxd wdt convw convb dtb alog dmat wout lng lnb".split()


def build(nc, ap, x, out, x1):
    fno_stage(nc, BATCH, x, x1, *[ap[n] for n in _FNO_ARGS])
    mamba_stage(nc, BATCH, x1, out, *[ap[n] for n in _MAMBA_ARGS])


def kernel(**inputs):
    import concourse.bacc as _bacc
    from concourse.bass_utils import run_bass_kernel_spmd as _run

    inputs = {k: np.asarray(v) for k, v in inputs.items()}
    arrays = {**fno_constants(), **mamba_constants(),
              **fno_weights(*[inputs["L0_conv_" + n] for n in _FNO]),
              **mamba_weights(*[inputs["L1_conv_" + n] for n in _MAMBA])}
    nc = _bacc.Bacc("TRN2", target_bir_lowering=False, num_devices=1)
    maps, ap = {}, {}
    for name, a in arrays.items():
        maps[f"in_{name}_dram"] = a
        ap[name] = nc.dram_tensor(f"in_{name}_dram", a.shape, mybir.dt.from_np(a.dtype), kind="ExternalInput").ap()
    shape = (BATCH, G * SC, H * H)
    maps["in_x_dram"] = np.ascontiguousarray(inputs["x"]).reshape(shape)
    x = nc.dram_tensor("in_x_dram", shape, F32, kind="ExternalInput").ap()
    x1 = nc.dram_tensor("x1_dram", shape, F32, kind="Internal").ap()
    out = nc.dram_tensor("out_0_dram", shape, F32, kind="ExternalOutput").ap()
    build(nc, ap, x, out, x1)
    r = _run(nc, [maps], core_ids=[0])
    return np.asarray(r.results[0]["out_0_dram"]).reshape(BATCH, G * SC, H, H)
```

```python
import concourse.bass as bass
from concourse import mybir
from contextlib import ExitStack
import numpy as np

F32 = mybir.dt.float32
BF16 = mybir.dt.bfloat16
ALU = mybir.AluOpType
ACT = mybir.ActivationFunctionType
AX = mybir.AxisListType

BATCH = 8
G = 4
SC = 2
WID = 10
MODES = 12
H = 256
HALF = H // 2
NLAYER = 4
KX = 2 * MODES
KY = MODES
QUAD = 32
CH = G * 2 * WID
PIX = HALF * H
BLOCK = 512
CHUNK = 4096
NCHUNK = PIX // CHUNK
NPAIR = PIX // (2 * BLOCK)
UNIT = 2048
ZBUF = 4
RCHUNK = 1024
SLOTS = [(0, 0), (0, 1), (0, 2), (1, 0), (1, 1), (2, 0)]
SROW = 2 * WID
STACK = len(SLOTS) * SROW
XQ = 64
HID = 128


def fno_stage(nc, ctx_nb, x, x1, grid, ident, gblk, gnsel, dfty, dftx, invy, invx,
              w0, wl, bl, betas_row, betas_free, wsp, w1f, b1t, w2f, b2t, wsel):
    NB = ctx_nb
    ctx = ExitStack()
    with ctx:
        def sb(name, shape, dt=F32):
            return ctx.enter_context(nc.sbuf_tensor(name, shape, dt))

        def sem(name):
            return ctx.enter_context(nc.semaphore(name))

        h = sb("h", [128, PIX])
        scratch = sb("scratch", [128, 2 * XQ * CH])
        Gs = sb("Gs", [128, 2, G * WID, 2 * KX])
        wmix = sb("wmix", [128, 2, WID, KY, WID])
        ident_s = sb("ident_s", [128, 128])
        dfty_s = sb("dfty_s", [128, 2, 2 * KX])
        dftx_s = sb("dftx_s", [128, 2, 2, 2 * KY])
        invy_s = sb("invy_s", [128, 2, H])
        gblk_s = sb("gblk_s", [128, 128])
        gnsel_s = sb("gnsel_s", [128, 2])
        w0_s = sb("w0_s", [128, CH])
        wl_s = sb("wl_s", [128, NLAYER, CH])
        z_last = sb("z_last", [128, 2 * BLOCK])
        w1_s = sb("w1_s", [128, 8, HID], BF16)
        wsel_s = sb("wsel_s", [128, 3])
        wcur = sb("wcur", [128, CH])
        bl_s = sb("bl_s", [128, NLAYER])
        spb = sb("spb", [128, NLAYER])
        beta_r = sb("beta_r", [128, 2 * NLAYER])
        sp_r = sb("sp_r", [128, 2 * NLAYER])
        inv_r = sb("inv_r", [128, NLAYER + 1])
        inv_q = sb("inv_q", [128, NLAYER + 1])
        beta_f = sb("beta_f", [128, G])
        sp_f = sb("sp_f", [128, G])
        inv_f = sb("inv_f", [128, G])
        b1_s = sb("b1_s", [128, G])
        b1sp = sb("b1sp", [128, G])
        b2_s = sb("b2_s", [128, 1])
        spt = sb("spt", [128, 6 * NLAYER])
        oc = sb("oc", [128, WID, QUAD])
        osn = sb("osn", [128, WID, QUAD])
        stats = sb("stats", [128, 8, 6])
        mv = sb("mv", [128, 2])
        dev = sb("dev", [128, 2])
        gn = sb("gn", [128, 4])
        gnm = sb("gnm", [128, 2])
        PS = ctx.enter_context(nc.psum_tensor("PSF", [128, 8, BLOCK], F32))

        hT = [scratch[:, q * XQ * CH:(q + 1) * XQ * CH].rearrange("p (x c) -> p x c", c=CH) for q in range(2)]
        xc = [scratch[:, q * CHUNK:(q + 1) * CHUNK] for q in range(2)]
        tmp = scratch[:, 0:WID * KY * 2 * WID].rearrange("p (o k r i) -> p o k r i", o=WID, k=KY, r=2)
        tmp_flat = scratch[:, 0:WID * KY * 2 * WID].rearrange("p (m r) -> p m r", r=2 * WID)
        rowW = scratch[:, 0:HALF * CH].rearrange("p (y c) -> p y c", c=CH)
        zflat = Gs[:, :, :, :].rearrange("p a c k -> p (a c k)")
        invx_s = zflat[:, 0:H]
        fr = zflat[:, 0:3 * WID * KY].rearrange("p (a i k) -> p a i k", a=3, i=WID)
        z = [zflat[:, 1024 * i:1024 * (i + 1)] for i in range(ZBUF - 1)] + [z_last[:, :]]
        wflat = wmix[:, :, :, :, :].rearrange("p r o k i -> p (r o k i)")
        pieces_h = [wflat[:, 0:UNIT // 2].bitcast(BF16), wflat[:, UNIT // 2:UNIT].bitcast(BF16)]

        def piece_last(u):
            if isinstance(u, int) and u == 0:
                return z_last[:, :].bitcast(BF16)
            return h[:, bass.ds((u - 1) * UNIT, UNIT // 2)].bitcast(BF16)

        stack = [scratch[:, q * (G * UNIT // 2):(q + 1) * (G * UNIT // 2)].bitcast(BF16).rearrange(
            "p (g f) -> p g f", g=G) for q in range(2)]
        xr = [scratch[:, G * UNIT + q * RCHUNK:G * UNIT + (q + 1) * RCHUNK] for q in range(2)]
        w1_raw, w1_acc, w1_b = [scratch[:, q * 8 * HID:(q + 1) * 8 * HID] for q in range(3)]
        w1_b = w1_b[:, 0:4 * HID].bitcast(BF16)
        w2_s = wflat[:, UNIT:UNIT + 8 * QUAD].rearrange("p (g m) -> p g m", m=QUAD)

        MIXROWS = WID * KY * 2 * WID // CH

        def bank(j, n=1):
            return PS[:, j:j + n, :].rearrange("p a b -> p (a b)")

        PAIR = [0, 4, 6]
        FBANK = 3
        GBANK = 4
        IBANKS = [4, 5, 6, 7, 0]

        const_in = sem("const_in")
        setup_v = sem("setup_v")
        setup_a = sem("setup_a")
        dense_in = sem("dense_in")
        st_part = sem("st_part")
        st_sum = sem("st_sum")
        st_v = sem("st_v")
        st_sqrt = sem("st_sqrt")
        xc_in = [sem("xc_in0"), sem("xc_in1")]
        xc_norm = sem("xc_norm")
        fc0_mm = sem("fc0_mm")
        h_written = sem("h_written")
        w_cur = sem("w_cur")
        wmix_in = sem("wmix_in")
        tr_ready = sem("tr_ready")
        tr_used = sem("tr_used")
        y_done = sem("y_done")
        g_used = sem("g_used")
        f_ready = sem("f_ready")
        f_copied = sem("f_copied")
        mixv = sem("mixv")
        o_ready = sem("o_ready")
        i_ready = sem("i_ready")
        s_act = sem("s_act")
        s_vec = sem("s_vec")
        w_rep = sem("w_rep")
        e_ready = sem("e_ready")
        w2_in = sem("w2_in")
        w2_scaled = sem("w2_scaled")
        xr_in = [sem("xr_in0"), sem("xr_in1")]
        piece_ready = sem("piece_ready")
        stack_in = sem("stack_in")
        w1_raw_in = sem("w1_raw_in")
        w1_step = sem("w1_step")
        z_mm = sem("z_mm")
        z_act = sem("z_act")
        z_used = sem("z_used")
        x1_done = sem("x1_done")
        x1_out = sem("x1_out")

        CONSTS = [(ident_s, ident), (dfty_s, dfty), (dftx_s, dftx), (invy_s, invy), (invx_s, invx),
                  (gblk_s, gblk), (gnsel_s, gnsel), (w0_s, w0), (wl_s, wl), (bl_s, bl),
                  (beta_r, betas_row), (beta_f, betas_free), (b1_s, b1t), (b2_s, b2t), (wsel_s, wsel)]
        x_dense = x.rearrange("b c (s f) -> b (c s) f", s=16)
        x_half = x.rearrange("b c (s f) -> b (c s) f", s=2)
        x1_half = x1.rearrange("b c (s f) -> b (c s) f", s=2)
        NUNIT = PIX // UNIT
        NRC = PIX // RCHUNK
        HPB = 5 * NPAIR
        START = 1
        AHEAD = 2
        block = ctx.enter_context(nc.Block())

        carrier = sem("carrier")

        def stand(eng):
            eng.sem_inc(carrier, 1)

        def full(t):
            return t[tuple([slice(None)] * len(t.shape))]

        @block.sync
        def _(sp):
            for t, src in CONSTS:
                sp.dma_start(full(t), src).then_inc(const_in, 16)
            sp.wait_ge(setup_v, 1)

            sp.dma_start(w1_raw, w1f).then_inc(w1_raw_in, 16)
            sp.wait_ge(setup_v, 9)

            with sp.Fori(0, NB) as b:
                sp.dma_start(xc[0], x_dense[b]).then_inc(dense_in, 16)
                sp.wait_ge(st_part, 2 * b + 1)
                for c in range(NCHUNK):
                    if c >= 2:
                        sp.wait_ge(fc0_mm, b * NPAIR + (c - 1) * 4)
                    for g in range(G):
                        sp.dma_start(xc[c % 2][QUAD * g:QUAD * g + 4, :],
                                     x_half[b, 4 * g:4 * g + 4, c * CHUNK:(c + 1) * CHUNK]).then_inc(xc_in[c % 2], 16)
                        sp.dma_start(xc[c % 2][QUAD * g + 4:QUAD * g + 8, :],
                                     grid[:, c * CHUNK:(c + 1) * CHUNK]).then_inc(xc_in[c % 2], 16)
                with sp.Fori(0, NLAYER) as l:
                    n = b * NLAYER + l
                    sp.wait_ge(o_ready, START + n)
                    stand(sp)
                    sp.wait_ge(z_used, ZBUF + b * (PIX // BLOCK * G))
                    sp.dma_start(wflat, wsp[l]).then_inc(wmix_in, 16)
                sp.wait_ge(o_ready, START + (b + 1) * NLAYER)
                sp.dma_start(w2_s.rearrange("p g m -> p (g m)"), w2f).then_inc(w2_in, 16)
                sp.wait_ge(h_written, START + (b + 1) * HPB)

                def move(u, piece):
                    held = pieces_h[piece] if piece < 2 else piece_last(u)
                    slots = [slot for slot, (hp, _) in enumerate(SLOTS) if hp == piece]
                    sp.wait_ge(piece_ready, b * (NUNIT * 4) + (4 * u + [1, 3, 4][piece]))
                    for slot in slots:
                        for g in range(G):
                            sp.dma_start(stack[u % 2][SROW * slot:SROW * (slot + 1), g, :],
                                         held[SROW * g:SROW * (g + 1), :]).then_inc(stack_in, 16)

                for piece in range(3):
                    move(0, piece)
                for u in range(1, NUNIT):
                    if u >= 2:
                        sp.wait_ge(z_mm, b * (PIX // BLOCK * G) + (u - 1) * (UNIT // BLOCK * G))
                        stand(sp)
                    for piece in range(3):
                        move(u, piece)
                sp.wait_ge(x1_out, (b + 1) * (NRC * G * 16))
                stand(sp)
            sp.wait_ge(x1_out, NB * NRC * G * 16)

        def pe_layer(pe, n, hbase):
            def transposes(q):
                for t in range(16 * q, 16 * q + 16):
                    if t >= 3:
                        pe.wait_ge(tr_used, n * 64 + t - 2)
                    for j in range(4):
                        xx = 4 * t + j
                        m = nc.tensor.transpose(bank(t % 3)[:, CH * j:CH * (j + 1)],
                                                h[0:CH, xx:xx + (HALF - 1) * H + 1:H], ident_s[0:CH, 0:CH])
                    m.then_inc(tr_ready, 1)

            def rows(q):
                pe.wait_ge(tr_used, n * 64 + 16 * (q + 1))
                if q == 2:
                    pe.wait_ge(g_used, n * 8 + 4)
                for ch in range(G * WID):
                    g, c = ch // WID, ch % WID
                    for yh in range(2):
                        col = (ch % WID) * 2 * KX
                        m = nc.tensor.matmul(
                            PS[XQ * (q % 2):XQ * (q % 2) + XQ, GBANK + g, col:col + 2 * KX],
                            hT[q % 2][:, :, g * 2 * WID + yh * WID + c], dfty_s[:, yh, :],
                            start=(yh == 0), stop=(yh == 1), skip_group_check=True)
                m.then_inc(y_done, 1)

            pe.wait_ge(h_written, START + hbase)
            transposes(0)
            transposes(1)
            rows(0)
            transposes(2)
            rows(1)
            transposes(3)
            rows(2)
            rows(3)
            pe.wait_ge(g_used, n * 8 + 8)
            for c in range(WID):
                for k, (xh, ri) in enumerate([(0, 0), (0, 1), (1, 0), (1, 1)]):
                    for g in range(G):
                        m = nc.tensor.matmul(
                            PS[QUAD * g:QUAD * g + KX, FBANK, c * 2 * KY:(c + 1) * 2 * KY],
                            Gs[:, xh, g * WID + c, ri * KX:(ri + 1) * KX], dftx_s[:, xh, ri, :],
                            start=(k == 0), stop=(k == 3), skip_group_check=True,
                            tile_position=(0, QUAD * g))
            m.then_inc(f_ready, 1)
            pe.wait_ge(o_ready, START + n + 1)
            stand(pe)
            for o in range(WID):
                for g in range(G):
                    q = slice(QUAD * g, QUAD * g + KX)
                    out = PS[QUAD * g:QUAD * (g + 1), IBANKS[o // 2], (o % 2) * H:(o % 2 + 1) * H]
                    nc.tensor.matmul(out, oc[q, o, :], invy_s[q, 0, :], start=True, stop=False,
                                     skip_group_check=True, tile_position=(QUAD * g, QUAD * g))
                    m = nc.tensor.matmul(out, osn[q, o, :], invy_s[q, 1, :], start=False, stop=True,
                                         skip_group_check=True, tile_position=(QUAD * g, QUAD * g))
                if o % 2:
                    m.then_inc(i_ready, 1)
            pe.wait_ge(w_rep, n + 1)
            pe.wait_ge(s_act, (n + 1) * 5)
            pe.wait_ge(s_vec, (n + 1) * 6)
            for k in range(NPAIR):
                if k >= 3:
                    pe.wait_ge(h_written, START + hbase + k - 2)
                for yy in range(4 * k, 4 * k + 4):
                    m = nc.tensor.matmul(PS[0:CH, PAIR[k % 3] + (yy // 2) % 2, (yy % 2) * H:(yy % 2 + 1) * H],
                                         rowW[:, yy, :], h[:, H * yy:H * (yy + 1)],
                                         start=True, stop=True)
                m.then_inc(e_ready, 1)

        @block.tensor
        def _(pe):
            pe.sem_inc(z_used, ZBUF)
            pe.wait_ge(const_in, 16 * len(CONSTS))
            pe.wait_ge(setup_v, 2)
            with pe.Fori(0, NB) as b:
                pe.wait_ge(x1_done, AHEAD + b * (PIX // BLOCK))
                pe.wait_ge(st_part, 2 * b + 1)
                nc.tensor.matmul(bank(0)[:, 0:1], gblk_s[:, :], mv[:, 0:1], start=True, stop=True).then_inc(st_sum, 1)
                pe.wait_ge(st_part, 2 * b + 2)
                nc.tensor.matmul(bank(0)[:, 1:2], gblk_s[:, :], dev[:, 1:2], start=True, stop=True).then_inc(st_sum, 1)
                pe.wait_ge(st_sqrt, b + 1)
                stand(pe)
                with pe.Fori(0, NCHUNK // 2) as cc:
                    for c in range(2):
                        pe.wait_ge(xc_norm, b * NCHUNK + cc * 2 + (c + 1))
                        for k in range(4):
                            if c == 0 and k < 3:
                                pe.wait_ge(h_written, START + b * HPB + cc * 8)
                            else:
                                pe.wait_ge(h_written, START + b * HPB + cc * 8 + (4 * c + k - 2))
                            p0 = PAIR[(4 * c + k) % 3]
                            for j in range(2):
                                m = nc.tensor.matmul(bank(p0 + j)[0:CH, :], w0_s[:, :],
                                                     xc[c][:, (2 * k + j) * BLOCK:(2 * k + j + 1) * BLOCK],
                                                     start=True, stop=True)
                            m.then_inc(fc0_mm, 1)
                with pe.Fori(0, NLAYER) as l:
                    pe_layer(pe, b * NLAYER + l, b * HPB + (l + 1) * NPAIR)
                pe.wait_ge(h_written, START + (b + 1) * HPB)
                pe.wait_ge(w2_scaled, b + 1)
                stand(pe)
                NBLK = PIX // BLOCK

                STEPS = 2 * (UNIT // BLOCK) * G

                def fc1(kk, i):
                    if i % (STEPS // 2) == 0:
                        pe.wait_ge(stack_in, (b * NUNIT + 2 * kk + (i // (STEPS // 2) + 1)) * (len(SLOTS) * G * 16))
                    pe.wait_ge(z_act, AHEAD + b * (NBLK * G) + kk * STEPS + i - 1)
                    blk, g = (i % (STEPS // 2)) // G, i % G
                    for yh in range(2):
                        m = nc.tensor.matmul(bank([0, 4][i % 2] + yh), w1_s[0:STACK, 2 * g + yh, :],
                                             stack[i // (STEPS // 2)][0:STACK, g, blk * BLOCK:(blk + 1) * BLOCK],
                                             start=True, stop=True)
                    m.then_inc(z_mm, 1)

                def fc2(kk, i):
                    zi = b * (NBLK * G) + kk * STEPS + i
                    blk = i // G
                    if i % G == 1:
                        pe.wait_ge(x1_done, AHEAD + b * NBLK + (kk * (STEPS // G) + blk - 1))
                    pe.wait_ge(z_act, AHEAD + zi + 1)
                    for yh in range(2):
                        for s in (i - 1, i):
                            g = s % G
                            m = nc.tensor.matmul(PS[QUAD * g:QUAD * (g + 1), 6 + blk % 2, :],
                                                 w2_s[:, 2 * g + yh, :],
                                                 z[s % ZBUF][:, yh * BLOCK:(yh + 1) * BLOCK],
                                                 start=(yh == 0), stop=(yh == 1),
                                                 skip_group_check=True, tile_position=(0, QUAD * g))
                            if yh == 1:
                                m.then_inc(z_used, 1)

                LAST = NUNIT // 2 - 1
                fc1(0, 0)
                fc1(0, 1)
                with pe.Fori(0, LAST) as kk:
                    for i in range(STEPS):
                        fc1(kk + (i + 2) // STEPS, (i + 2) % STEPS)
                        if i % 2:
                            fc2(kk, i)
                for i in range(STEPS):
                    if i + 2 < STEPS:
                        fc1(LAST, i + 2)
                    if i % 2:
                        fc2(LAST, i)

        def mixed_rows(j, g):
            return PS[QUAD * g:QUAD * (g + 1), IBANKS[j], :].rearrange("p (o h y) -> p o h y", o=2, h=2)

        def row_spectrum(j, g):
            return rowW[96:128, :, 2 * WID * g:2 * WID * (g + 1)].rearrange(
                "p y (h o) -> p o h y", h=2)[:, 2 * j:2 * j + 2, :, :]

        def act_layer(act, n, l, hbase, last):
            act.wait_ge(h_written, START + hbase)
            stand(act)
            nc.scalar.copy(wcur[:, :], wl_s[:, bass.ds(l, 1), :].rearrange("p a m -> p (a m)")).then_inc(w_cur, 1)
            for xh in range(2):
                act.wait_ge(y_done, n * 4 + 2 * xh + 2)
                for g in range(4):
                    nc.scalar.copy(
                        Gs[:, xh, g * WID:(g + 1) * WID, :].rearrange("p c k -> p (c k)"),
                        PS[:, GBANK + g, 0:WID * 2 * KX]).then_inc(g_used, 1)
            act.wait_ge(f_ready, n + 1)
            stand(act)
            fv = PS[:, FBANK, 0:WID * 2 * KY].rearrange("p (c r k) -> p r c k", r=2, k=KY)
            for part in range(2):
                nc.scalar.activation(fr[:, part, :, :], fv[:, part, :, :], ACT.Copy,
                                     scale=inv_q[:, bass.ds(l, 1)]).then_inc(f_copied, 1)
            for j in range(5):
                act.wait_ge(i_ready, n * 5 + j + 1)
                nc.scalar.copy(row_spectrum(j, 0), mixed_rows(j, 0))
                nc.scalar.copy(row_spectrum(j, 1), mixed_rows(j, 1)).then_inc(s_act, 1)
            for k in range(NPAIR):
                act.wait_ge(e_ready, n * NPAIR + k + 1)
                stand(act)
                out = h[0:CH, 2 * BLOCK * k:2 * BLOCK * (k + 1)]
                if last:
                    nc.scalar.activation(out, bank(PAIR[k % 3], 2)[0:CH, :], ACT.Identity,
                                         bias=bl_s[0:CH, NLAYER - 1:NLAYER]).then_inc(h_written, 1)
                else:
                    nc.scalar.activation(out, bank(PAIR[k % 3], 2)[0:CH, :], ACT.Silu, scale=sp_r[0:CH, bass.ds(l, 1)],
                                         bias=spb[0:CH, bass.ds(l, 1)]).then_inc(h_written, 1)

        @block.scalar
        def _(act):
            act.sem_inc(h_written, START)
            act.sem_inc(z_act, AHEAD)
            act.wait_ge(const_in, 16 * len(CONSTS))
            act.wait_ge(setup_v, 3)
            nc.scalar.activation(spt[:, 12:24], spt[:, 0:12], ACT.Exp, scale=-1.0).then_inc(setup_a, 1)
            act.wait_ge(setup_a, 1)
            nc.scalar.activation(spt[:, 12:24], spt[:, 12:24], ACT.Ln, bias=1.0).then_inc(setup_a, 1)
            act.wait_ge(setup_v, 9)
            with act.Fori(0, NB) as b:
                act.wait_ge(st_v, (b + 1) * 3)
                nc.scalar.activation(gn[:, 2:3], gn[:, 1:2], ACT.Sqrt).then_inc(st_sqrt, 1)
                with act.Fori(0, NPAIR // 8) as kk:
                    for k in range(8):
                        act.wait_ge(fc0_mm, b * NPAIR + kk * 8 + (k + 1))
                        stand(act)
                        nc.scalar.copy(h[0:CH, bass.ds(kk * (16 * BLOCK) + k * 2 * BLOCK, 2 * BLOCK)],
                                       bank(PAIR[k % 3], 2)[0:CH, :]).then_inc(h_written, 1)
                with act.Fori(0, NLAYER - 1) as l:
                    act_layer(act, b * NLAYER + l, l, b * HPB + (l + 1) * NPAIR, False)
                act_layer(act, b * NLAYER + (NLAYER - 1), NLAYER - 1, b * HPB + NLAYER * NPAIR, True)
                NBLK = PIX // BLOCK
                with act.Fori(0, NBLK // 2) as kk:
                    for i in range(2 * G):
                        g = i % G
                        act.wait_ge(z_mm, b * (NBLK * G) + kk * (2 * G) + i + 1)
                        act.wait_ge(z_used, b * (NBLK * G) + kk * (2 * G) + i + 1)
                        nc.scalar.activation(z[i % ZBUF], bank([0, 4][i % 2], 2), ACT.Silu,
                                             scale=sp_f[:, g:g + 1], bias=b1sp[:, g:g + 1]).then_inc(z_act, 1)

        @block.gpsimd
        def _(pool):
            with pool.Fori(0, NB) as b:
                with pool.Fori(0, NLAYER) as l:
                    n = b * NLAYER + l
                    pool.wait_ge(w_cur, n + 1)
                    pool.wait_ge(y_done, n * 4 + 4)
                    stand(pool)
                    nc.gpsimd.tensor_copy(rowW[0:96, MIXROWS:HALF, :],
                                          wcur[0:96, None, :].to_broadcast([96, HALF - MIXROWS, CH])).then_inc(w_rep, 1)

                pool.wait_ge(h_written, START + (b + 1) * HPB)
                stand(pool)

                def load(c):
                    if c >= 2:
                        pool.wait_ge(x1_out, b * (NRC * G * 16) + (c - 1) * G * 16)
                        stand(pool)
                    for g in range(G):
                        pool.dma_start(xr[c % 2][QUAD * g:QUAD * g + 4, :],
                                     x_half[b, 4 * g:4 * g + 4, c * RCHUNK:(c + 1) * RCHUNK]).then_inc(xr_in[c % 2], 16)

                def store(c):
                    pool.wait_ge(x1_done, AHEAD + b * (PIX // BLOCK) + (c + 1) * (RCHUNK // BLOCK))
                    stand(pool)
                    for g in range(G):
                        pool.dma_start(x1_half[b, 4 * g:4 * g + 4, c * RCHUNK:(c + 1) * RCHUNK],
                                     xr[c % 2][QUAD * g:QUAD * g + 4, :]).then_inc(x1_out, 16)

                load(0)
                load(1)
                for c in range(NRC):
                    store(c)
                    if c + 2 < NRC:
                        load(c + 2)

        @block.vector
        def _(v):
            v.sem_inc(o_ready, START)
            v.sem_inc(x1_done, AHEAD)
            v.memset(scratch[:, :], 0.0).then_inc(setup_v, 1)
            v.memset(PS[:, FBANK, :], 0.0)
            v.memset(oc[:, :, :], 0.0)
            v.memset(osn[:, :, :], 0.0).then_inc(setup_v, 1)
            v.wait_ge(const_in, 16 * len(CONSTS))
            v.scalar_tensor_tensor(spt[:, 0:8], beta_r[:, :], -1.0, beta_r[:, :], ALU.mult, ALU.max)
            v.scalar_tensor_tensor(spt[:, 8:12], beta_f[:, :], -1.0, beta_f[:, :], ALU.mult, ALU.max).then_inc(setup_v, 1)
            v.wait_ge(setup_a, 2)
            v.scalar_tensor_tensor(sp_r[:, :], beta_r[:, :], 0.0, spt[:, 12:20], ALU.max, ALU.add).then_inc(setup_v, 1)
            v.scalar_tensor_tensor(sp_f[:, :], beta_f[:, :], 0.0, spt[:, 20:24], ALU.max, ALU.add).then_inc(setup_v, 1)
            v.wait_ge(setup_v, 5)
            v.tensor_scalar(sp_r[:, :], sp_r[:, :], 1e-30, None, ALU.max)
            v.tensor_scalar(sp_f[:, :], sp_f[:, :], 1e-30, None, ALU.max).then_inc(setup_v, 1)
            v.wait_ge(setup_v, 6)
            v.tensor_tensor(spb[:, :], sp_r[:, 0:NLAYER], bl_s[:, :], ALU.mult)
            v.tensor_tensor(b1sp[:, :], sp_f[:, :], b1_s[:, :], ALU.mult)
            v.tensor_scalar(spt[:, 0:8], sp_r[:, :], 1.1, None, ALU.mult)
            v.tensor_scalar(spt[:, 8:12], sp_f[:, :], 1.1, None, ALU.mult).then_inc(setup_v, 1)
            v.wait_ge(setup_v, 7)
            v.memset(inv_r[:, 0:1], 1.0)
            v.memset(inv_q[:, 0:1], 1.0)
            v.reciprocal(inv_r[:, 1:1 + NLAYER], spt[:, 0:4])
            v.reciprocal(inv_q[:, 1:1 + NLAYER], spt[:, 4:8])
            v.reciprocal(inv_f[:, :], spt[:, 8:12]).then_inc(setup_v, 1)
            v.wait_ge(setup_v, 8)
            for l in range(1, NLAYER):
                v.tensor_scalar(wl_s[:, l, :], wl_s[:, l, :], inv_r[:, l:l + 1], None, ALU.mult)
            v.tensor_copy(h[64:128, :].rearrange("p (y x) -> p y x", x=H),
                          invx_s[64:128, None, :].to_broadcast([64, HALF, H]))
            v.memset(stats[:, :, :], 0.0)
            v.wait_ge(w1_raw_in, 16)
            w1_flat = w1_s.rearrange("p g m -> p (g m)")
            done = 0
            for piece in range(3):
                v.tensor_copy(w1_b, w1_raw).then_inc(w1_step, 1)
                v.wait_ge(w1_step, done + 1)
                if piece == 0:
                    v.tensor_scalar(w1_acc, w1_b, wsel_s[:, 0:1], None, ALU.mult)
                else:
                    v.scalar_tensor_tensor(w1_acc, w1_b, wsel_s[:, piece:piece + 1], w1_acc, ALU.mult, ALU.add)
                v.tensor_tensor(w1_raw, w1_raw, w1_b, ALU.subtract).then_inc(w1_step, 1)
                v.wait_ge(w1_step, done + 2)
                done += 2
            v.tensor_copy(w1_flat, w1_acc).then_inc(setup_v, 1)
            v.wait_ge(setup_v, 9)
            with v.Fori(0, NB) as b:
                v.wait_ge(dense_in, (b + 1) * 16)
                for j in range(8):
                    m = v.bn_stats(stats[:, j, :], xc[0][:, j * 512:(j + 1) * 512])
                m.then_inc(st_v, 1)
                v.wait_ge(st_v, b * 3 + 1)
                stand(v)
                v.bn_aggr(mv[:, :], stats[:, :, :].rearrange("p a b -> p (a b)")).then_inc(st_part, 1)
                v.wait_ge(st_part, 2 * b + 1)
                v.wait_ge(st_sum, 2 * b + 1)
                v.tensor_copy(gn[:, 0:1], bank(0)[:, 0:1])
                v.tensor_tensor(dev[:, 0:1], mv[:, 0:1], bank(0)[:, 0:1], ALU.subtract).then_inc(st_v, 1)
                v.wait_ge(st_v, b * 3 + 2)
                v.scalar_tensor_tensor(dev[:, 1:2], dev[:, 0:1], dev[:, 0:1], mv[:, 1:2],
                                       ALU.mult, ALU.add).then_inc(st_part, 1)
                v.wait_ge(st_sum, 2 * b + 2)
                v.tensor_scalar(gn[:, 1:2], bank(0)[:, 1:2], 1e-5, None, ALU.add).then_inc(st_v, 1)
                v.wait_ge(st_sqrt, b + 1)
                v.reciprocal(gn[:, 3:4], gn[:, 2:3])
                v.tensor_scalar(gnm[:, 0:1], gn[:, 0:1], gnsel_s[:, 0:1], None, ALU.mult).then_inc(mixv, 1)
                v.wait_ge(mixv, (b * (2 + 8 * NLAYER)) + 1)
                v.tensor_scalar(gnm[:, 1:2], gn[:, 3:4], gnsel_s[:, 0:1], gnsel_s[:, 1:2],
                                ALU.mult, ALU.add).then_inc(mixv, 1)
                v.wait_ge(mixv, (b * (2 + 8 * NLAYER)) + 2)
                stand(v)
                with v.Fori(0, NCHUNK // 2) as cc:
                    for c in range(2):
                        v.wait_ge(xc_in[c], (b * (NCHUNK // 2) + cc + 1) * (2 * G * 16))
                        v.tensor_scalar(xc[c], xc[c], gnm[:, 0:1], gnm[:, 1:2], ALU.subtract,
                                        ALU.mult).then_inc(xc_norm, 1)
                with v.Fori(0, NLAYER) as l:
                    n = b * NLAYER + l
                    for t in range(64):
                        if t == 32 or t == 48:
                            v.wait_ge(y_done, n * 4 + (t // 16 - 1))
                        v.wait_ge(tr_ready, n * 64 + t + 1)
                        src = bank(t % 3)[:, 0:4 * CH].rearrange("p (x c) -> p x c", c=CH)
                        x0 = 4 * (t % 16)
                        dst = hT[(t // 16) % 2][:, x0:x0 + 4, :]
                        v.tensor_copy(dst, src).then_inc(tr_used, 1)
                    v.wait_ge(f_copied, n * 2 + 2)
                    mv0 = b * (2 + 8 * NLAYER) + 2 + l * 8
                    v.tensor_scalar(fr[:, 2, :, :], fr[:, 1, :, :], -1.0, None, ALU.mult).then_inc(mixv, 1)
                    v.wait_ge(mixv, mv0 + 1)
                    v.wait_ge(wmix_in, (n + 1) * 16)

                    def product(slot, w_part, f_part):
                        f = fr[:, f_part, :, :].rearrange("p i k -> p k i")
                        f = f[:, None, :, :].to_broadcast([128, WID, KY, WID])
                        return v.tensor_tensor(tmp[:, :, :, slot, :], wmix[:, w_part, :, :, :], f, ALU.mult)

                    def gather(part):
                        return v.tensor_reduce(oc[:, :, part * KY:(part + 1) * KY],
                                               tmp_flat.rearrange("p (o k) r -> p o k r", o=WID),
                                               AX.X, ALU.add)
                    product(0, 0, 0)
                    product(1, 1, 2).then_inc(mixv, 1)
                    v.wait_ge(mixv, mv0 + 2)
                    gather(0).then_inc(mixv, 1)
                    v.wait_ge(mixv, mv0 + 3)
                    product(0, 0, 1)
                    product(1, 1, 0).then_inc(mixv, 1)
                    v.wait_ge(mixv, mv0 + 4)
                    gather(1).then_inc(mixv, 1)
                    v.wait_ge(mixv, mv0 + 5)
                    v.tensor_scalar(osn[:, :, 0:KY], oc[:, :, KY:2 * KY], -1.0, None, ALU.mult).then_inc(mixv, 1)
                    v.tensor_copy(osn[:, :, KY:2 * KY], oc[:, :, 0:KY]).then_inc(mixv, 1)
                    v.wait_ge(mixv, mv0 + 7)
                    v.nop().then_inc(o_ready, 1)
                    v.nop().then_inc(mixv, 1)
                    v.wait_ge(w_cur, n + 1)
                    v.tensor_copy(rowW[0:96, 0:MIXROWS, :],
                                  wcur[0:96, None, :].to_broadcast([96, MIXROWS, CH])).then_inc(s_vec, 1)
                    for j in range(5):
                        v.wait_ge(i_ready, n * 5 + j + 1)
                        v.tensor_copy(row_spectrum(j, 2), mixed_rows(j, 2))
                        v.tensor_copy(row_spectrum(j, 3), mixed_rows(j, 3)).then_inc(s_vec, 1)
                v.wait_ge(w2_in, (b + 1) * 16)
                for g in range(G):
                    m = v.tensor_scalar(w2_s[:, 2 * g:2 * g + 2, :], w2_s[:, 2 * g:2 * g + 2, :],
                                        inv_f[:, g:g + 1], None, ALU.mult)
                m.then_inc(w2_scaled, 1)
                NBLK = PIX // BLOCK

                def split_step(u, step):
                    hu = h[0:CH, bass.ds(u * UNIT, UNIT)]
                    p0, p1, p2 = [p[0:CH, :] for p in (*pieces_h, piece_last(u))]
                    if step == 0:
                        v.wait_ge(stack_in, (b * NUNIT + u) * (len(SLOTS) * G * 16))
                    else:
                        v.wait_ge(piece_ready, b * (NUNIT * 4) + u * 4 + step)
                    stand(v)
                    if step == 0:
                        m = v.tensor_copy(p0, hu)
                    elif step == 1:
                        m = v.tensor_tensor(hu, hu, p0, ALU.subtract)
                    elif step == 2:
                        m = v.tensor_copy(p1, hu)
                    else:
                        m = v.tensor_tensor(p2, hu, p1, ALU.subtract)
                    m.then_inc(piece_ready, 1)

                def residual(u, k):
                    c = k // 2
                    if k % 2 == 0:
                        v.wait_ge(xr_in[c], (b * NUNIT + u + 1) * (G * 16))
                    v.wait_ge(z_used, ZBUF + G * (b * NBLK + u * (UNIT // BLOCK) + (k + 1)))
                    blk = xr[c][:, (k % 2) * BLOCK:(k % 2 + 1) * BLOCK]
                    v.scalar_tensor_tensor(blk, bank(6 + k % 2), b2_s[:, 0:1], blk, ALU.add,
                                           ALU.add).then_inc(x1_done, 1)

                v.wait_ge(h_written, START + b * HPB + (HPB - NPAIR + UNIT // (2 * BLOCK)))
                for step in range(4):
                    split_step(0, step)
                with v.Fori(0, NUNIT - 1) as u:
                    split_step(u + 1, 0)
                    split_step(u + 1, 1)
                    residual(u, 0)
                    split_step(u + 1, 2)
                    split_step(u + 1, 3)
                    for k in range(1, UNIT // BLOCK):
                        residual(u, k)
                for k in range(UNIT // BLOCK):
                    residual(NUNIT - 1, k)


def fno_constants():
    f = np.float32
    c = {}
    kx = np.concatenate([np.arange(MODES), np.arange(H - MODES, H)])
    ky = np.arange(KY)
    y = np.arange(H)
    lin = np.linspace(0.0, 1.0, H).astype(f)
    grid = np.zeros((4, HALF, H), f)
    grid[0] = lin[:HALF, None]
    grid[1] = lin[HALF:, None]
    grid[2] = lin[None, :]
    grid[3] = 1.0
    c["grid"] = grid.reshape(4, PIX)
    c["ident"] = np.eye(128, dtype=f)
    c["gblk"] = (np.kron(np.eye(G), np.ones((QUAD, QUAD))) / QUAD).astype(f)
    sel = np.zeros((128, 2), f)
    for g in range(G):
        sel[QUAD * g:QUAD * g + 4, 0] = 1
        sel[QUAD * g + 4:QUAD * g + 8, 1] = 1
    c["gnsel"] = sel
    a = 2 * np.pi * (np.outer(y, kx) % H) / H
    c["dfty"] = np.concatenate([np.cos(a), -np.sin(a)], 1).reshape(2, HALF, 2 * KX).transpose(1, 0, 2).astype(f)
    a = 2 * np.pi * (np.outer(y, ky) % H) / H
    cs, sn = np.cos(a), np.sin(a)
    dx = np.stack([np.concatenate([cs, -sn], 1), np.concatenate([sn, cs], 1)], 1)
    c["dftx"] = dx.reshape(2, HALF, 2, 2 * KY).transpose(1, 0, 2, 3).astype(f)
    iy = np.zeros((G, QUAD, 2, H))
    a = 2 * np.pi * (np.outer(kx, y) % H) / H
    iy[:, :KX, 0] = np.cos(a)
    iy[:, :KX, 1] = np.sin(a)
    c["invy"] = iy.reshape(128, 2, H).astype(f)
    ix = np.zeros((128, H))
    wt = np.where(ky == 0, 1.0, 2.0)[:, None] / (H * H)
    a = 2 * np.pi * (np.outer(ky, y) % H) / H
    ix[96:96 + KY] = wt * np.cos(a)
    ix[96 + KY:96 + 2 * KY] = -wt * np.sin(a)
    c["invx"] = ix.astype(f)
    return {k: np.ascontiguousarray(v) for k, v in c.items()}


def fno_weights(fc0_w, fc0_b, w_w, w_b, sp_w1, sp_w2, betas, fc1_w, fc1_b, fc2_w, fc2_b):
    f = np.float32
    c = {}
    w0 = np.zeros((128, CH), f)
    wl = np.zeros((128, NLAYER, CH), f)
    bl = np.zeros((128, NLAYER), f)
    rows = np.zeros((128, NLAYER), f)
    w1 = np.zeros((128, 8, HID), f)
    wsel = np.zeros((128, 3), f)
    for slot, (_, piece) in enumerate(SLOTS):
        wsel[SROW * slot:SROW * (slot + 1), piece] = 1
    w2 = np.zeros((HID, 8, QUAD), f)
    b2 = np.zeros((128, 1), f)
    for g in range(G):
        for yh in range(2):
            cols = slice(2 * WID * g + WID * yh, 2 * WID * g + WID * (yh + 1))
            rows[cols] = betas[:, g]
            for i in range(SC):
                w0[QUAD * g + 2 * i + yh, cols] = fc0_w[g, :, i]
                w2[:, 2 * g + yh, 2 * i + yh] = fc2_w[g, i]
                b2[QUAD * g + 2 * i + yh, 0] = fc2_b[SC * g + i]
            w0[QUAD * g + 4 + yh, cols] = fc0_w[g, :, SC]
            w0[QUAD * g + 6, cols] = fc0_w[g, :, SC + 1]
            w0[QUAD * g + 7, cols] = fc0_b[WID * g:WID * (g + 1)]
            wl[cols, :, cols] = w_w[:, g].transpose(2, 0, 1)
            bl[cols] = w_b[:, WID * g:WID * (g + 1)].T
            for slot in range(len(SLOTS)):
                lo = SROW * slot + WID * yh
                w1[lo:lo + WID, 2 * g + yh] = fc1_w[g].T
    c["wsel"] = wsel
    c["w0"], c["wl"], c["bl"], c["w1f"], c["w2f"], c["b2t"] = w0, wl, bl, w1.reshape(128, -1), w2.reshape(128, -1), b2
    c["betas_row"] = np.concatenate([rows, np.repeat(betas.T, QUAD, axis=0)], axis=1)
    c["betas_free"] = np.broadcast_to(betas[NLAYER - 1], (128, G))
    c["b1t"] = fc1_b.reshape(G, HID).T
    sp = np.concatenate([sp_w1, sp_w2], axis=4)
    full = np.zeros((NLAYER, G, QUAD, 2, WID, KY, WID), f)
    full[:, :, :KX] = sp.transpose(0, 1, 4, 6, 3, 5, 2)
    c["wsp"] = full.reshape(NLAYER, 128, 2 * WID * KY * WID)
    return {k: np.ascontiguousarray(v) for k, v in c.items()}


R = 4
DM = 128
DI = 256
NS = 64
DTR = 8
KC = 4
L = (H // R) * (H // R)
TC = 1024
NTC = L // TC
RPC = TC * R // H * R
SB = 32
PIECES = 3
BK = 512


def mamba_stage(nc, NB, x1, out, ident, gblk, gmap, ones, sel, win, wx, wxd, wdt, convw, convb,
                dtb, alog, dmat, wout, lng, lnb):
    ctx = ExitStack()
    with ctx:
        def sb(name, shape, dt=F32):
            return ctx.enter_context(nc.sbuf_tensor(name, shape, dt))

        def sem(name):
            return ctx.enter_context(nc.semaphore(name))

        ident_m = sb("ident_m", [128, 128])
        gblk_m = sb("gblk_m", [128, 128])
        gmap_m = sb("gmap_m", [128, 128])
        ones_m = sb("ones_m", [128, 128])
        sel_m = sb("sel_m", [PIECES * SB, SB, 128], BF16)
        win_m = sb("win_m", [128, 4, 128])
        wx_m = sb("wx_m", [128, 2, 128])
        wxd_m = sb("wxd_m", [128, 2, DTR])
        wdt_m = sb("wdt_m", [DTR, 2, 128])
        convw_m = sb("convw_m", [128, 2, KC])
        convb_m = sb("convb_m", [128, 2])
        dtb_m = sb("dtb_m", [128, 2])
        a_log = sb("a_log", [128, SB, 4])
        a_neg = sb("a_neg", [128, SB, 4])
        dmat_m = sb("dmat_m", [128, 2, 128])
        wout_m = sb("wout_m", [128, 2, 128])
        lng_m = sb("lng_m", [128, 1])
        lnb_m = sb("lnb_m", [128, 1])
        eps = sb("eps", [128, 1])
        zero16 = sb("zero16", [1, BK], BF16)
        shuf = sb("shuf", [128, R * TC])
        u = sb("u", [128, TC])
        xg = sb("xg", [128, TC])
        xres = sb("xres", [128, TC])
        cen = sb("cen", [128, TC])
        sq = sb("sq", [128, TC])
        fin = sb("fin", [128, TC])
        xpad = sb("xpad", [128, 2, KC - 1 + TC])
        ta = sb("ta", [128, 2, TC])
        tb = sb("tb", [128, 2, TC])
        xs = sb("xs", [128, 2, TC])
        sz = sb("sz", [128, 2, TC])
        dt_ = sb("dt_", [128, 2, TC])
        dtx = sb("dtx", [128, 2, TC])
        dtl = sb("dtl", [DTR, TC])
        pieces = sb("pieces", [128, PIECES, TC], BF16)
        bcp = sb("bcp", [PIECES * SB, 4, TC], BF16)
        decay = sb("decay", [128, 4, TC])
        drive = sb("drive", [128, 2, TC])
        hs = sb("hs", [128, 4, TC])
        hc = sb("hc", [128, 4, TC])
        cb = sb("cb", [128, 2, TC])
        carry = sb("carry", [128, SB, 4])
        stats = sb("stats_m", [128, 8, 6])
        mv = sb("mv_m", [128, 2])
        dev = sb("dev_m", [128, 2])
        gn = sb("gn_m", [128, 4])
        gnt = sb("gnt", [128, BATCH, 2])
        logs = sb("logs", [128, 2, TC])
        PS = ctx.enter_context(nc.psum_tensor("PSM", [128, 8, BK], F32))

        def bank(j, n=2):
            return PS[:, j:j + n, :].rearrange("p a b -> p (a b)")

        xa, xd, fo, oi = (shuf[QUAD * i:QUAD * (i + 1), :] for i in range(4))

        sel_in_f32 = shuf[0:PIECES * SB, :]
        CONSTS = [(ident_m, ident), (gblk_m, gblk), (gmap_m, gmap), (ones_m, ones), (sel_in_f32, sel),
                  (win_m, win), (wx_m, wx), (wxd_m, wxd), (wdt_m, wdt), (convw_m, convw),
                  (convb_m, convb), (dtb_m, dtb), (a_log, alog), (dmat_m, dmat), (wout_m, wout),
                  (lng_m, lng), (lnb_m, lnb)]
        const_in = sem("mconst_in")
        setup_v = sem("msetup_v")
        setup_a = sem("msetup_a")
        dense_in = sem("mdense_in")
        bn_done = sem("bn_done")
        st_part = sem("mst_part")
        st_sum = sem("mst_sum")
        dev_done = sem("dev_done")
        var_ready = sem("var_ready")
        st_sqrt = sem("mst_sqrt")
        gn_ready = sem("gn_ready")
        xa_in = sem("xa_in")
        deint = sem("deint")
        u_in = sem("u_in")
        xres_ready = sem("xres_ready")
        xg_ready = sem("xg_ready")
        z_mm = sem("mz_mm")
        z_ev = sem("z_ev")
        mean_mm = sem("mean_mm")
        cen_ready = sem("cen_ready")
        sq_ready = sem("sq_ready")
        var_mm = sem("var_mm")
        var_ev = sem("var_ev")
        std_ready = sem("std_ready")
        rstd_ready = sem("rstd_ready")
        un_half = sem("un_half")
        un_ready = sem("un_ready")
        pad_zero = sem("pad_zero")
        pad_front = sem("pad_front")
        xin_mm = sem("xin_mm")
        xin_ev = sem("xin_ev")
        tap = sem("tap")
        sz_ready = sem("sz_ready")
        xs_ready = sem("xs_ready")
        bc_mm = sem("bc_mm")
        split = sem("split")
        bcp_in = sem("bcp_in")
        dtl_mm = sem("dtl_mm")
        dtl_ev = sem("dtl_ev")
        dt_mm = sem("dt_mm")
        v_ev = sem("v_ev")
        abs_ready = sem("abs_ready")
        e_ready = sem("me_ready")
        ln_ready = sem("ln_ready")
        spstep = sem("spstep")
        dt_ready = sem("dt_ready")
        dtx_ready = sem("dtx_ready")
        b_ready = sem("b_ready")
        c_ready = sem("c_ready")
        c_copied = sem("c_copied")
        bx_done = sem("bx_done")
        a_ready = sem("a_ready")
        scan_done = sem("scan_done")
        hc_done = sem("hc_done")
        red_done = sem("red_done")
        carried = sem("carried")
        zeroed = sem("zeroed")
        y_ready = sem("y_ready")
        gated = sem("gated")
        out_mm = sem("out_mm")
        fin_ready = sem("fin_ready")
        fo_in = sem("fo_in")
        il_done = sem("il_done")
        out_done = sem("out_done")

        x_dense = x1.rearrange("b c (s f) -> b (c s) f", s=16)

        def image_rows(t, b, c):
            return t.rearrange("b c (n h r w) -> b n c r h w", n=NTC, r=R, w=H)[b, c]

        AHEAD = 4
        EARLY = 4
        START = 1
        PREP = 7
        block = ctx.enter_context(nc.Block())
        carrier = sem("mcarrier")

        def stand(eng):
            eng.sem_inc(carrier, 1)

        def full(t):
            return t[tuple([slice(None)] * len(t.shape))]

        def half(j):
            return slice(j * BK, (j + 1) * BK)

        def chunks(eng, body):
            with eng.Fori(0, NB) as b:
                with eng.Fori(0, NTC - 1) as c:
                    body(b * NTC + c, b, c, b, c + 1, False)
                body(b * NTC + (NTC - 1), b, NTC - 1, (b + 1) % NB, 0, True)

        @block.sync
        def _(sp):
            sp.sem_inc(u_in, START)
            sp.sem_inc(fo_in, START)
            sp.sem_inc(out_done, START)
            for t, src in CONSTS:
                sp.dma_start(full(t), src).then_inc(const_in, 16)
            sp.wait_ge(setup_v, 1)
            with sp.Fori(0, NB) as b:
                sp.dma_start(shuf[:, :], x_dense[b]).then_inc(dense_in, 16)
                sp.wait_ge(bn_done, b + 1)
                stand(sp)

            def load_rows(n, b, c):
                src = image_rows(x1, b, c)
                sp.wait_ge(deint, START + n)
                stand(sp)
                for ch in range(8):
                    sp.dma_start(xa[R * ch:R * (ch + 1), :].rearrange("p (h w) -> p h w", w=H),
                                 src[ch]).then_inc(xa_in, 16)

            def load_tokens(n, xres_of):
                sp.wait_ge(deint, START + n + 1)
                stand(sp)
                if xres_of is not None:
                    sp.wait_ge(xres_ready, xres_of + 1)
                for r in range(R):
                    sp.dma_start(u[QUAD * r:QUAD * (r + 1), :], xd[:, r * TC:(r + 1) * TC]).then_inc(u_in, 16)

            def load_blocks(n):
                sp.wait_ge(split, (n + 1) * 8)
                sp.wait_ge(c_copied, START + n * (4 * SB))
                for j in range(4):
                    for p in range(PIECES):
                        sp.dma_start(bcp[SB * p:SB * (p + 1), j, :],
                                     pieces[SB * j:SB * (j + 1), p, :]).then_inc(bcp_in, 16)

            load_rows(0, 0, 0)
            load_tokens(0, None)
            load_blocks(0)

            def body(k, b, c, bn, cn, new_image):
                n = k + 1
                load_rows(n, bn, cn)
                load_tokens(n, k)
                load_blocks(n)
                sp.wait_ge(fin_ready, START + (k + 1) * 2)
                for r in range(R):
                    sp.dma_start(fo[:, r * TC:(r + 1) * TC], fin[QUAD * r:QUAD * (r + 1), :]).then_inc(fo_in, 16)
                sp.wait_ge(il_done, k + 1)
                dst = image_rows(out, b, c)
                for ch in range(8):
                    sp.dma_start(dst[ch],
                                 oi[R * ch:R * (ch + 1), :].rearrange("p (h w) -> p h w", w=H)).then_inc(out_done, 16)
            chunks(sp, body)
            sp.wait_ge(out_done, START + NB * NTC * 16 * 8)

        @block.tensor
        def _(pe):
            def b_row(n, r, jb):
                pe.wait_ge(bx_done, START + n * (4 * SB) + (4 * r + 2 * jb))
                for j in range(2):
                    m = nc.tensor.matmul(PS[:, 4 + j, :], sel_m[:, r, :], bcp[:, jb, half(j)], start=True, stop=True)
                m.then_inc(b_ready, 1)

            def c_row(n, r, jb, j):
                pe.wait_ge(c_copied, START + n * (4 * SB) + (4 * r + 2 * jb + j))
                nc.tensor.matmul(PS[:, 6, :], sel_m[:, r, :], bcp[:, 2 + jb, half(j)],
                                 start=True, stop=True).then_inc(c_ready, 1)

            def add_up(n, r, jb, dh):
                i = 2 * jb + dh
                pe.wait_ge(hc_done, n * (4 * SB) + (4 * r + i + 1 + AHEAD))
                for j in range(2):
                    m = nc.tensor.matmul(PS[:, 2 * dh + j, :], ident_m[:, :], hc[:, i, half(j)],
                                         start=False, stop=False, skip_group_check=True)
                m.then_inc(red_done, 1)

            def group(n, r, jb, added):
                b_row(n, r, jb)
                for j in range(2):
                    c_row(n, r, jb, j)
                    if added is not None:
                        add_up(*added, j)

            def iteration(n, r):
                group(n, r, 0, (n, r - 1, 0))
                group(n, r, 1, (n, r - 1, 1))

            def product(pairs, rows=128):
                for i, (w, d) in enumerate(pairs):
                    m = nc.tensor.matmul(PS[0:rows, PREP, :], w, d, start=(i == 0), stop=(i == len(pairs) - 1))
                return m

            def z(k, i):
                if i == 0:
                    pe.wait_ge(fin_ready, START + k * 2)
                else:
                    pe.wait_ge(z_ev, START + k * 4 + i)
                product([(win_m[:, 2 + i // 2, :], cen[:, half(i % 2)])]).then_inc(z_mm, 1)

            def mean(n, j):
                if j == 0:
                    pe.wait_ge(z_ev, START + n * 4)
                    pe.wait_ge(xg_ready, n + 1)
                else:
                    pe.wait_ge(cen_ready, n * 2 + 1)
                product([(ones_m[:, :], xg[:, half(j)])]).then_inc(mean_mm, 1)

            def var(n, j):
                pe.wait_ge(cen_ready, n * 2 + 2)
                pe.wait_ge(sq_ready, n * 2 + j + 1)
                if j == 1:
                    pe.wait_ge(var_ev, n * 2 + 1)
                product([(ones_m[:, :], sq[:, half(j)])]).then_inc(var_mm, 1)

            def xin(n, i):
                if i == 0:
                    pe.wait_ge(var_ev, n * 2 + 2)
                    pe.wait_ge(un_ready, n + 1)
                else:
                    pe.wait_ge(xin_ev, n * 4 + i)
                product([(win_m[:, i // 2, :], cen[:, half(i % 2)])]).then_inc(xin_mm, 1)

            def bc(n, j):
                if j == 0:
                    pe.wait_ge(xin_ev, n * 4 + 4)
                    pe.wait_ge(xs_ready, n * 2 + 2)
                else:
                    pe.wait_ge(split, n * 8 + 2)
                product([(wx_m[:, dh, :], xs[:, dh, half(j)]) for dh in range(2)]).then_inc(bc_mm, 1)

            def dtl_step(n, j):
                if j == 0:
                    pe.wait_ge(split, n * 8 + 6)
                else:
                    pe.wait_ge(dtl_ev, n * 2 + 1)
                product([(wxd_m[:, dh, :], xs[:, dh, half(j)]) for dh in range(2)], DTR).then_inc(dtl_mm, 1)

            def dt_step(n, i):
                if i == 0:
                    pe.wait_ge(dtl_ev, n * 2 + 2)
                else:
                    pe.wait_ge(v_ev, n * 4 + i)
                product([(wdt_m[:, i // 2, :], dtl[:, half(i % 2)])]).then_inc(dt_mm, 1)

            def out_step(k, j):
                if j == 0:
                    pe.wait_ge(v_ev, k * 4 + 8)
                    pe.wait_ge(gated, START + k * 2 + 2)
                else:
                    pe.wait_ge(fin_ready, START + k * 2 + 1)
                product([(wout_m[:, dh, :], ta[:, dh, half(j)]) for dh in range(2)]).then_inc(out_mm, 1)

            def switch(k, n):
                pe.wait_ge(bcp_in, (n + 1) * (12 * 16))
                for jb in range(2):
                    group(n, 0, jb, None if k is None else (k, SB - 1, jb))
                if k is not None:
                    for j in range(4):
                        m = nc.tensor.matmul(PS[:, j, :], zero16[:, 0:128], zero16[:, :], start=False, stop=True,
                                             skip_group_check=True)
                    m.then_inc(y_ready, 1)
                group(n, 1, 0, None)
                pe.wait_ge(gated, START + n * 2)
                for i in range(4):
                    nc.tensor.matmul(PS[:, i, :], dmat_m[:, i // 2, :], xs[:, i // 2, half(i % 2)],
                                     start=True, stop=False, skip_group_check=True)
                for dh in range(2):
                    add_up(n, 0, 0, dh)
                if k is not None:
                    out_step(k, 0)
                group(n, 1, 1, (n, 0, 1))
                if k is not None:
                    out_step(k, 1)
                for r in range(2, EARLY):
                    iteration(n, r)

            pe.wait_ge(const_in, 16 * len(CONSTS))
            pe.wait_ge(setup_v, 1)
            pe.sem_inc(red_done, AHEAD)
            with pe.Fori(0, NB) as b:
                pe.wait_ge(st_part, 2 * b + 1)
                nc.tensor.matmul(PS[:, 0, 0:1], gblk_m[:, :], mv[:, 0:1], start=True, stop=True)
                nc.tensor.matmul(PS[:, 0, 2:3], gmap_m[:, :], mv[:, 0:1], start=True, stop=True).then_inc(st_sum, 1)
                pe.wait_ge(st_part, 2 * b + 2)
                nc.tensor.matmul(PS[:, 0, 4:5], gmap_m[:, :], dev[:, 1:2], start=True, stop=True).then_inc(st_sum, 1)
            pe.wait_ge(gn_ready, NB)
            for j in range(2):
                mean(0, j)
            for j in range(2):
                var(0, j)
            for i in range(4):
                xin(0, i)
            for j in range(2):
                bc(0, j)
            for j in range(2):
                dtl_step(0, j)
            for i in range(4):
                dt_step(0, i)
            switch(None, 0)

            def body(k, b, c, bn, cn, new_image):
                n = k + 1
                after = {4: (z, k, 0), 5: (z, k, 1), 6: (z, k, 2), 7: (z, k, 3), 8: (mean, n, 0), 9: (mean, n, 1),
                         10: (var, n, 0), 11: (var, n, 1), 13: (xin, n, 0), 14: (xin, n, 1), 15: (xin, n, 2),
                         16: (xin, n, 3), 19: (bc, n, 0), 20: (bc, n, 1), 21: (dtl_step, n, 0),
                         22: (dtl_step, n, 1), 23: (dt_step, n, 0), 24: (dt_step, n, 1), 25: (dt_step, n, 2),
                         26: (dt_step, n, 3)}
                for r in range(EARLY, SB):
                    iteration(k, r)
                    if r in after:
                        step, *of = after[r]
                        step(*of)
                switch(k, n)
            chunks(pe, body)

        @block.scalar
        def _(act):
            act.sem_inc(c_copied, START)
            act.sem_inc(z_ev, START)
            act.sem_inc(deint, START)
            act.sem_inc(carried, 2)

            def group(n, r, jb):
                for dh in range(2):
                    i = 2 * jb + dh
                    act.wait_ge(scan_done, n * (4 * SB) + (4 * r + i + 1))
                    nc.scalar.activation(decay[:, i, :], dt_[:, dh, :], ACT.Exp,
                                         scale=a_neg[:, r, i:i + 1]).then_inc(a_ready, 1)
                    act.wait_ge(c_ready, n * (4 * SB) + (4 * r + 2 * jb + dh + 1))
                    if dh == 0:
                        act.wait_ge(hc_done, n * (4 * SB) + (4 * r + 2 * jb + 2))
                    nc.scalar.copy(cb[:, jb, half(dh)], PS[:, 6, :]).then_inc(c_copied, 1)

            def keep(n, r, jb):
                act.wait_ge(scan_done, n * (4 * SB) + (4 * r + 2 * jb + 2 + AHEAD))
                nc.scalar.copy(carry[:, r, 2 * jb:2 * jb + 2].rearrange("p (a b) -> p a b", b=1),
                               hs[:, 2 * jb:2 * jb + 2, TC - 1:TC]).then_inc(carried, 1)

            def iteration(n, r):
                group(n, r, 0)
                keep(n, r - 1, 1)
                group(n, r, 1)
                keep(n, r, 0)

            def deinterleave(n):
                act.wait_ge(xa_in, (n + 1) * (16 * 8))
                act.wait_ge(u_in, START + n * 64)
                nc.scalar.copy(xd.rearrange("p (r t) -> p r t", r=R),
                               xa.rearrange("p (t r) -> p r t", r=R)).then_inc(deint, 1)

            def z_copy(k, i):
                act.wait_ge(z_mm, k * 4 + i + 1)
                if i == 0:
                    act.wait_ge(gated, START + k * 2)
                nc.scalar.copy(sz[:, i // 2, half(i % 2)], PS[:, PREP, :]).then_inc(z_ev, 1)

            def square(n, j):
                act.wait_ge(cen_ready, n * 2 + j + 1)
                nc.scalar.activation(sq[:, half(j)], cen[:, half(j)], ACT.Square).then_inc(sq_ready, 1)

            def var_copy(n):
                act.wait_ge(var_mm, n * 2 + 1)
                nc.scalar.copy(sq[:, half(0)], PS[:, PREP, :]).then_inc(var_ev, 1)

            def std(n):
                act.wait_ge(var_mm, n * 2 + 2)
                nc.scalar.activation(sq[:, half(1)], PS[:, PREP, :], ACT.Sqrt, bias=eps[:, 0:1]).then_inc(var_ev, 1)
                act.wait_ge(var_ev, n * 2 + 1)
                nc.scalar.activation(sq[:, half(0)], sq[:, half(0)], ACT.Sqrt, bias=eps[:, 0:1]).then_inc(std_ready, 1)

            def front(n, images):
                if images is not None:
                    act.wait_ge(pad_zero, images)
                act.wait_ge(tap, START + n * 8)
                nc.scalar.copy(xpad[:, :, 0:KC - 1], xpad[:, :, TC:TC + KC - 1]).then_inc(pad_front, 1)

            def xin_copy(n, i):
                if i == 0:
                    act.wait_ge(pad_front, n + 1)
                act.wait_ge(xin_mm, n * 4 + i + 1)
                lo = KC - 1 + (i % 2) * BK
                nc.scalar.copy(xpad[:, i // 2, lo:lo + BK], PS[:, PREP, :]).then_inc(xin_ev, 1)

            def first_tap(n, dh):
                act.wait_ge(xin_ev, n * 4 + 2 * dh + 2)
                if dh == 1:
                    act.wait_ge(tap, START + n * 8 + 4)
                nc.scalar.activation(ta[:, dh, :], xpad[:, dh, 0:TC], ACT.Copy,
                                     scale=convw_m[:, dh, 0:1]).then_inc(tap, 1)

            def silu_x(n):
                for dh in range(2):
                    act.wait_ge(tap, START + n * 8 + 4 * (dh + 1))
                    nc.scalar.activation(xs[:, dh, :], ta[:, dh, :], ACT.Silu, bias=convb_m[:, dh:dh + 1]).then_inc(xs_ready, 1)

            def silu_z(k):
                act.wait_ge(z_ev, START + k * 4 + 4)
                nc.scalar.activation(sz[:, :, :], sz[:, :, :], ACT.Silu).then_inc(sz_ready, 1)

            def dtl_copy(n, j):
                act.wait_ge(dtl_mm, n * 2 + j + 1)
                nc.scalar.copy(dtl[:, half(j)], PS[0:DTR, PREP, :]).then_inc(dtl_ev, 1)

            def v_copy(n, i):
                act.wait_ge(dt_mm, n * 4 + i + 1)
                nc.scalar.activation(ta[:, i // 2, half(i % 2)], PS[:, PREP, :], ACT.Identity,
                                     bias=dtb_m[:, i // 2:i // 2 + 1]).then_inc(v_ev, 1)

            def exp_ln(n):
                act.wait_ge(split, n * 8 + 8)
                act.wait_ge(v_ev, n * 4 + 4)
                nc.scalar.activation(tb[:, :, :], ta[:, :, :], ACT.Abs).then_inc(abs_ready, 1)
                act.wait_ge(abs_ready, n + 1)
                nc.scalar.activation(tb[:, :, :], tb[:, :, :], ACT.Exp, scale=-1.0).then_inc(e_ready, 1)
                act.wait_ge(e_ready, n + 1)
                nc.scalar.activation(logs[:, :, :], tb[:, :, :], ACT.Ln, bias=1.0).then_inc(ln_ready, 1)

            def interleave(k):
                act.wait_ge(fo_in, START + (k + 1) * 64)
                act.wait_ge(out_done, START + k * (16 * 8))
                nc.scalar.copy(oi.rearrange("p (t r) -> p r t", r=R),
                               fo.rearrange("p (r t) -> p r t", r=R)).then_inc(il_done, 1)

            def switch(k, n):
                if k is not None:
                    keep(k, SB - 1, 1)
                act.wait_ge(dt_ready, n + 1)
                group(n, 0, 0)
                group(n, 0, 1)
                keep(n, 0, 0)
                for r in range(1, EARLY):
                    iteration(n, r)
                if k is not None:
                    interleave(k)

            act.wait_ge(const_in, 16 * len(CONSTS))
            nc.scalar.activation(a_neg[:, :, :], a_log[:, :, :], ACT.Exp).then_inc(setup_a, 1)
            act.wait_ge(setup_v, 2)
            with act.Fori(0, NB) as b:
                act.wait_ge(var_ready, b + 1)
                nc.scalar.activation(gn[:, 2:3], gn[:, 1:2], ACT.Sqrt).then_inc(st_sqrt, 1)
            deinterleave(0)
            for j in range(2):
                square(0, j)
            var_copy(0)
            std(0)
            front(0, None)
            for i in range(4):
                xin_copy(0, i)
            first_tap(0, 0)
            first_tap(0, 1)
            silu_x(0)
            for j in range(2):
                dtl_copy(0, j)
            for i in range(4):
                v_copy(0, i)
            exp_ln(0)
            switch(None, 0)

            def body(k, b, c, bn, cn, new_image):
                n = k + 1
                after = {4: [(deinterleave, n)], 5: [(z_copy, k, 0)], 6: [(z_copy, k, 1)], 7: [(z_copy, k, 2)],
                         8: [(z_copy, k, 3)], 10: [(square, n, 0)], 11: [(square, n, 1), (var_copy, n)],
                         12: [(std, n)], 13: [(front, n, b + 1 if new_image else None)], 14: [(xin_copy, n, 0)],
                         15: [(xin_copy, n, 1), (first_tap, n, 0)], 16: [(xin_copy, n, 2)], 17: [(xin_copy, n, 3), (first_tap, n, 1)],
                         19: [(silu_x, n), (silu_z, k)], 22: [(dtl_copy, n, 0)], 23: [(dtl_copy, n, 1)],
                         24: [(v_copy, n, 0)], 25: [(v_copy, n, 1)], 26: [(v_copy, n, 2)], 27: [(v_copy, n, 3)],
                         29: [(exp_ln, n)]}
                for r in range(EARLY, SB):
                    iteration(k, r)
                    for step, *of in after.get(r, []):
                        step(*of)
                switch(k, n)
            chunks(act, body)

        @block.gpsimd
        def _(pool):
            pool.sem_inc(hc_done, AHEAD)
            def iteration(q):
                for jb in range(2):
                    for dh in range(2):
                        i = 2 * jb + dh
                        pool.wait_ge(scan_done, q * 4 + (i + 1 + AHEAD))
                        if dh == 0:
                            pool.wait_ge(c_copied, START + q * 4 + (2 * jb + 2))
                        pool.wait_ge(red_done, q * 4 + (i + 1))
                        nc.gpsimd.tensor_tensor(hc[:, i, :], hs[:, i, :], cb[:, jb, :], ALU.mult).then_inc(hc_done, 1)
            with pool.Fori(0, NB * NTC * SB + EARLY) as q:
                iteration(q)

        @block.vector
        def _(v):
            def iteration(n, r):
                for jb in range(2):
                    t0 = n * (4 * SB)
                    i0 = 4 * r + 2 * jb
                    v.wait_ge(b_ready, n * (2 * SB) + (2 * r + jb + 1))
                    for dh in range(2):
                        v.wait_ge(scan_done, t0 + (i0 + dh - 1 + AHEAD))
                        v.tensor_tensor(drive[:, dh, :], dtx[:, dh, :], bank(4), ALU.mult).then_inc(bx_done, 1)
                    for dh in range(2):
                        i = 2 * jb + dh
                        v.wait_ge(bx_done, START + t0 + (i0 + dh + 1))
                        v.wait_ge(a_ready, t0 + (i0 + dh + 1))
                        v.wait_ge(hc_done, t0 + (i0 + dh + 1))
                        v.wait_ge(carried, n * (2 * SB) + (2 * r + jb + 1))
                        v.tensor_tensor_scan(hs[:, i, :], decay[:, i, :], drive[:, dh, :], carry[:, r, i:i + 1],
                                             ALU.mult, ALU.add).then_inc(scan_done, 1)

            def residual(k):
                v.wait_ge(fin_ready, START + k * 2)
                v.wait_ge(xg_ready, k + 1)
                v.tensor_tensor(xres[:, :], xg[:, :], u[:, :], ALU.add).then_inc(xres_ready, 1)

            def group_norm(n, bn):
                v.wait_ge(u_in, START + (n + 1) * 64)
                stand(v)
                stat = gnt[:, bass.ds(bn, 1), :].rearrange("p a s -> p (a s)") if bn is not None else gnt[:, 0, :]
                v.tensor_scalar(xg[:, :], u[:, :], stat[:, 0:1], stat[:, 1:2], ALU.subtract, ALU.mult).then_inc(xg_ready, 1)

            def centre(n, j):
                v.wait_ge(mean_mm, n * 2 + j + 1)
                v.tensor_tensor(cen[:, half(j)], xg[:, half(j)], PS[:, PREP, :], ALU.subtract).then_inc(cen_ready, 1)

            def rstd(n):
                v.wait_ge(std_ready, n + 1)
                v.wait_ge(var_ev, n * 2 + 2)
                v.reciprocal(sq[:, :], sq[:, :]).then_inc(rstd_ready, 1)

            def normalise(n):
                v.wait_ge(rstd_ready, n + 1)
                v.scalar_tensor_tensor(cen[:, :], cen[:, :], lng_m[:, 0:1], sq[:, :], ALU.mult, ALU.mult).then_inc(un_half, 1)
                v.wait_ge(un_half, n + 1)
                v.tensor_scalar(cen[:, :], cen[:, :], lnb_m[:, 0:1], None, ALU.add).then_inc(un_ready, 1)

            def zero_pad(n):
                v.wait_ge(pad_front, n)
                v.memset(xpad[:, :, TC:TC + KC - 1], 0.0).then_inc(pad_zero, 1)

            def convolve(n, dh):
                v.wait_ge(xin_ev, n * 4 + 2 * dh + 2)
                for t in range(1, KC):
                    v.wait_ge(tap, START + n * 8 + (4 * dh + t))
                    v.scalar_tensor_tensor(ta[:, dh, :], xpad[:, dh, t:t + TC], convw_m[:, dh, t:t + 1],
                                           ta[:, dh, :], ALU.mult, ALU.add).then_inc(tap, 1)

            def pieces_of(n, j):
                p, rest = PS[:, PREP, :], tb[:, 0, half(j)]
                s0 = n * 8 + 4 * j
                v.wait_ge(bc_mm, n * 2 + j + 1)
                if j == 0 and not isinstance(n, int):
                    v.wait_ge(bcp_in, n * (12 * 16))
                v.tensor_copy(pieces[:, 0, half(j)], p).then_inc(split, 1)
                v.wait_ge(split, s0 + 1)
                v.tensor_tensor(rest, p, pieces[:, 0, half(j)], ALU.subtract).then_inc(split, 1)
                v.wait_ge(split, s0 + 2)
                v.tensor_copy(pieces[:, 1, half(j)], rest).then_inc(split, 1)
                v.wait_ge(split, s0 + 3)
                v.tensor_tensor(pieces[:, 2, half(j)], rest, pieces[:, 1, half(j)], ALU.subtract).then_inc(split, 1)

            def softplus(n, dh):
                v.wait_ge(ln_ready, n + 1)
                if dh == 1:
                    v.wait_ge(spstep, n * 6 + 3)
                v.tensor_scalar(sq[:, :], tb[:, dh, :], 1.0, 1.0, ALU.add, ALU.subtract).then_inc(spstep, 1)
                v.scalar_tensor_tensor(ta[:, dh, :], ta[:, dh, :], 0.0, logs[:, dh, :], ALU.max, ALU.add).then_inc(spstep, 1)
                v.wait_ge(spstep, n * 6 + 3 * dh + 1)
                v.tensor_tensor(tb[:, dh, :], tb[:, dh, :], sq[:, :], ALU.subtract).then_inc(spstep, 1)

            def steps_of_dt(n):
                v.wait_ge(spstep, n * 6 + 6)
                v.tensor_tensor(dt_[:, :, :], ta[:, :, :], tb[:, :, :], ALU.add).then_inc(dt_ready, 1)
                v.wait_ge(dt_ready, n + 1)
                v.tensor_tensor(dtx[:, :, :], dt_[:, :, :], xs[:, :, :], ALU.mult).then_inc(dtx_ready, 1)
                v.wait_ge(dtx_ready, n + 1)
                stand(v)

            def gate(k):
                v.wait_ge(y_ready, k + 1)
                v.wait_ge(sz_ready, k + 1)
                for dh in range(2):
                    v.tensor_tensor(ta[:, dh, :], sz[:, dh, :], bank(2 * dh), ALU.mult).then_inc(gated, 1)

            def result(k, j):
                v.wait_ge(out_mm, k * 2 + j + 1)
                v.wait_ge(xres_ready, k + 1)
                if j == 0:
                    v.wait_ge(fo_in, START + k * 64)
                v.tensor_tensor(fin[:, half(j)], xres[:, half(j)], PS[:, PREP, :], ALU.add).then_inc(fin_ready, 1)

            def switch(k, n, images):
                if k is not None:
                    v.wait_ge(scan_done, n * (4 * SB) + AHEAD)
                steps_of_dt(n)
                if images is not None:
                    v.wait_ge(carried, n * (2 * SB) + 2)
                    v.memset(carry[:, :, :], 0.0).then_inc(zeroed, 1)
                    v.wait_ge(zeroed, images)
                    stand(v)
                iteration(n, 0)
                if k is not None:
                    gate(k)
                iteration(n, 1)
                if k is not None:
                    result(k, 0)
                iteration(n, 2)
                if k is not None:
                    result(k, 1)
                for r in range(3, EARLY):
                    iteration(n, r)

            v.sem_inc(tap, START)
            v.sem_inc(gated, START)
            v.sem_inc(fin_ready, START)
            v.sem_inc(bx_done, START)
            v.memset(zero16[:, :], 0.0)
            v.wait_ge(const_in, 16 * len(CONSTS))
            v.tensor_copy(sel_m[:, :, :].rearrange("p r m -> p (r m)"), sel_in_f32).then_inc(setup_v, 1)
            v.memset(xpad[:, :, TC:TC + KC - 1], 0.0)
            v.memset(eps[:, :], 1e-5)
            v.wait_ge(setup_a, 1)
            v.tensor_scalar(a_neg[:, :, :], a_neg[:, :, :], -1.0, None, ALU.mult).then_inc(setup_v, 1)
            v.sem_inc(scan_done, AHEAD)
            with v.Fori(0, NB) as b:
                v.wait_ge(dense_in, (b + 1) * 16)
                for j in range(8):
                    m = v.bn_stats(stats[:, j, :], shuf[:, j * 512:(j + 1) * 512])
                m.then_inc(bn_done, 1)
                v.wait_ge(bn_done, b + 1)
                stand(v)
                v.bn_aggr(mv[:, :], stats[:, :, :].rearrange("p a b -> p (a b)")).then_inc(st_part, 1)
                v.wait_ge(st_part, 2 * b + 1)
                v.wait_ge(st_sum, 2 * b + 1)
                v.tensor_tensor(dev[:, 0:1], mv[:, 0:1], PS[:, 0, 0:1], ALU.subtract).then_inc(dev_done, 1)
                v.tensor_copy(gnt[:, bass.ds(b, 1), 0:1].rearrange("p a s -> p (a s)"), PS[:, 0, 2:3])
                v.wait_ge(dev_done, b + 1)
                v.scalar_tensor_tensor(dev[:, 1:2], dev[:, 0:1], dev[:, 0:1], mv[:, 1:2],
                                       ALU.mult, ALU.add).then_inc(st_part, 1)
                v.wait_ge(st_sum, 2 * b + 2)
                v.tensor_scalar(gn[:, 1:2], PS[:, 0, 4:5], 1e-5, None, ALU.add).then_inc(var_ready, 1)
                v.wait_ge(st_sqrt, b + 1)
                stand(v)
                v.reciprocal(gnt[:, bass.ds(b, 1), 1:2].rearrange("p a s -> p (a s)"), gn[:, 2:3]).then_inc(gn_ready, 1)
            v.wait_ge(gn_ready, NB)
            group_norm(0, None)
            for j in range(2):
                centre(0, j)
            rstd(0)
            normalise(0)
            for dh in range(2):
                convolve(0, dh)
            for j in range(2):
                pieces_of(0, j)
            for dh in range(2):
                softplus(0, dh)
            switch(None, 0, 1)

            def body(k, b, c, bn, cn, new_image):
                n = k + 1
                after = {4: [(residual, k)], 6: [(group_norm, n, bn)], 9: [(centre, n, 0)], 10: [(centre, n, 1)],
                         12: [(rstd, n)], 13: [(normalise, n)], 16: [(convolve, n, 0)], 18: [(convolve, n, 1)],
                         20: [(pieces_of, n, 0)], 21: [(pieces_of, n, 1)], 30: [(softplus, n, 0)], 31: [(softplus, n, 1)]}
                if new_image:
                    after[11] = [(zero_pad, n)]
                for r in range(EARLY, SB):
                    iteration(k, r)
                    for step, *of in after.get(r, []):
                        step(*of)
                switch(k, n, b + 2 if new_image else None)
            chunks(v, body)


def mamba_constants():
    f = np.float32
    c = {}
    c["ones"] = np.full((128, 128), 1.0 / DM, f)
    gp = np.repeat(np.arange(G), 32)
    gu = np.tile(np.repeat(np.arange(G), 8), R)
    c["gmap"] = ((gp[:, None] == gu[None, :]) / 32.0).astype(f)
    sel = np.zeros((PIECES, SB, SB, 128), f)
    for r in range(SB):
        sel[:, r, r, :] = 1
    c["sel"] = sel.reshape(PIECES * SB, SB * 128)
    return {k: np.ascontiguousarray(v) for k, v in c.items()}


def mamba_weights(ln_gamma, ln_beta, in_proj_w, conv_w, conv_b, x_proj_w, dt_proj_w, dt_proj_b, A_log, D, out_proj_w):
    f = np.float32
    c = {}
    perm = np.arange(DM).reshape(8, R, R).transpose(2, 0, 1).reshape(-1)
    c["win"] = in_proj_w[:, perm].T.reshape(DM, 4, 128)
    c["wx"] = x_proj_w[DTR:].T.reshape(2, 128, 128).transpose(1, 0, 2)
    c["wxd"] = x_proj_w[:DTR].T.reshape(2, 128, DTR).transpose(1, 0, 2)
    c["wdt"] = dt_proj_w.T.reshape(DTR, 2, 128)
    c["convw"] = conv_w.reshape(2, 128, KC).transpose(1, 0, 2)
    c["convb"] = conv_b.reshape(2, 128).T
    c["dtb"] = dt_proj_b.reshape(2, 128).T
    c["alog"] = A_log.reshape(2, 128, 2, SB).transpose(1, 3, 2, 0).reshape(128, SB, 4)
    dm = np.zeros((128, 2, 128), f)
    for dh in range(2):
        dm[np.arange(128), dh, np.arange(128)] = D[128 * dh:128 * (dh + 1)]
    c["dmat"] = dm
    c["wout"] = out_proj_w[perm].T.reshape(2, 128, 128).transpose(1, 0, 2)
    c["lng"] = ln_gamma[perm][:, None]
    c["lnb"] = ln_beta[perm][:, None]
    return {k: np.ascontiguousarray(v) for k, v in c.items()}


_FNO = "fc0_w fc0_b w_w w_b sp_w1 sp_w2 betas fc1_w fc1_b fc2_w fc2_b".split()
_MAMBA = "ln_gamma ln_beta in_proj_w conv_w conv_b x_proj_w dt_proj_w dt_proj_b A_log D out_proj_w".split()
_FNO_ARGS = "grid ident gblk gnsel dfty dftx invy invx w0 wl bl betas_row betas_free wsp w1f b1t w2f b2t wsel".split()
_MAMBA_ARGS = "ident gblk gmap ones sel win wx wxd wdt convw convb dtb alog dmat wout lng lnb".split()


def build(nc, ap, x, out, x1):
    fno_stage(nc, BATCH, x, x1, *[ap[n] for n in _FNO_ARGS])
    mamba_stage(nc, BATCH, x1, out, *[ap[n] for n in _MAMBA_ARGS])


def kernel(**inputs):
    import concourse.bacc as _bacc
    from concourse.bass_utils import run_bass_kernel_spmd as _run

    inputs = {k: np.asarray(v) for k, v in inputs.items()}
    arrays = {**fno_constants(), **mamba_constants(),
              **fno_weights(*[inputs["L0_conv_" + n] for n in _FNO]),
              **mamba_weights(*[inputs["L1_conv_" + n] for n in _MAMBA])}
    nc = _bacc.Bacc("TRN2", target_bir_lowering=False, num_devices=1)
    maps, ap = {}, {}
    for name, a in arrays.items():
        maps[f"in_{name}_dram"] = a
        ap[name] = nc.dram_tensor(f"in_{name}_dram", a.shape, mybir.dt.from_np(a.dtype), kind="ExternalInput").ap()
    shape = (BATCH, G * SC, H * H)
    maps["in_x_dram"] = np.ascontiguousarray(inputs["x"]).reshape(shape)
    x = nc.dram_tensor("in_x_dram", shape, F32, kind="ExternalInput").ap()
    x1 = nc.dram_tensor("x1_dram", shape, F32, kind="Internal").ap()
    out = nc.dram_tensor("out_0_dram", shape, F32, kind="ExternalOutput").ap()
    build(nc, ap, x, out, x1)
    r = _run(nc, [maps], core_ids=[0])
    return np.asarray(r.results[0]["out_0_dram"]).reshape(BATCH, G * SC, H, H)
```
